# Optimizing a Trainium2 kernel written in Bass

```python
import numpy as np
import jax
import jax.numpy as jnp

def _softmax(x, axis=-1):
    return jax.nn.softmax(x, axis=axis)

def _gelu(x):
    return jax.nn.gelu(x, approximate=True)

def _silu(x):
    return jax.nn.silu(x)

def _sigmoid(x):
    return jax.nn.sigmoid(x)

def _layernorm(x, axis=-1, eps=1e-05):
    m = jnp.mean(x, axis=axis, keepdims=True)
    v = jnp.var(x, axis=axis, keepdims=True)
    return (x - m) / jnp.sqrt(v + eps)

def _scatter_add(tgt, idx, src, axis=0):
    return tgt.at[idx].add(src)

def _segment_sum(src, seg, n):
    return jax.ops.segment_sum(src, seg, n)
kernel_name = 'mk_xattn_ffn_d1_seqx_r8_7afb2b'

def setup_inputs(seed: int=0):
    np.random.seed(seed)
    _w = jnp.asarray

    def _rec_inputs():
        import jax
        import jax.numpy as jnp
        _rk = jax.random.key(seed)
        x = -0.0003929 + 0.9999 * jax.random.normal(jax.random.fold_in(_rk, 1), (4, 512, 128), jnp.float32)
        _lenS = 512 - jax.random.randint(jax.random.fold_in(_rk, 7), (4,), 0, max(1, 512 // 4) + 1, jnp.int32)
        _lenS2 = 77 - jax.random.randint(jax.random.fold_in(_rk, 8), (4,), 0, max(1, 77 // 4) + 1, jnp.int32)
        _ctx_1024P = jax.random.normal(jax.random.fold_in(_rk, 11), (4, 16, 128), jnp.float32)
        _ctx_1024c = jax.random.dirichlet(jax.random.fold_in(_rk, 511), 0.3 * jnp.ones((16,), jnp.float32), (4, 77))
        _ctx_1024t = jnp.einsum('bsk,bkd->bsd', _ctx_1024c, _ctx_1024P)
        _ctx_1024t = _ctx_1024t * jax.lax.rsqrt(jnp.mean(jnp.square(_ctx_1024t)) + 1e-12) * 0.953939
        ctx_1024 = 2.81802e-05 + 1.00001 * (_ctx_1024t + 0.3 * jax.random.normal(jax.random.fold_in(_rk, 611), (4, 77, 128), jnp.float32))
        return (x, ctx_1024)
    x, ctx_1024 = _rec_inputs()

    def _L0_xattn_setup():
        import jax, jax.numpy as jnp
        import numpy as np
        D = 128
        key = jax.random.key(seed)
        ks = jax.random.split(key, 9)
        B, Nq, Nk = (8, 256, 256)
        s = 1.0 / np.sqrt(D)
        return {'query': jax.random.normal(ks[0], (B, Nq, D), jnp.float32), 'key': jax.random.normal(ks[1], (B, Nk, D), jnp.float32), 'value': jax.random.normal(ks[2], (B, Nk, D), jnp.float32), 'Wq': jax.random.uniform(ks[3], (D, D), jnp.float32, -s, s), 'bq': jax.random.uniform(ks[4], (D,), jnp.float32, -s, s), 'Wk': jax.random.uniform(ks[5], (D, D), jnp.float32, -s, s), 'bk': jax.random.uniform(ks[6], (D,), jnp.float32, -s, s), 'Wv': jax.random.uniform(ks[7], (D, D), jnp.float32, -s, s), 'bv': jax.random.uniform(ks[8], (D,), jnp.float32, -s, s)}
    _L0_xattn_all = _L0_xattn_setup()
    _L0_xattn_in = {k: v for k, v in _L0_xattn_all.items() if k in ('Wq', 'bq', 'Wk', 'bk', 'Wv', 'bv')}
    del _L0_xattn_all

    def _L0_ffn_setup():
        import jax, jax.numpy as jnp
        import numpy as np
        HIDDEN = 128
        INTER = 256
        NUM_EXPERTS = 8
        TOPK = 2
        STD = 0.02
        key = jax.random.key(seed)
        k1, k2, k3, k4 = jax.random.split(key, 4)
        return {'hidden_states': jax.random.normal(k1, (1, 256, HIDDEN), dtype=jnp.float32), 'w1': jax.random.normal(k2, (NUM_EXPERTS, 2 * INTER, HIDDEN), dtype=jnp.float32) * STD, 'w2': jax.random.normal(k3, (NUM_EXPERTS, HIDDEN, INTER), dtype=jnp.float32) * STD, 'router_w': jax.random.normal(k4, (NUM_EXPERTS, HIDDEN), dtype=jnp.float32) * STD}
    _L0_ffn_all = _L0_ffn_setup()
    _L0_ffn_in = {k: v for k, v in _L0_ffn_all.items() if k in ('w1', 'w2', 'router_w')}
    del _L0_ffn_all
    return {'x': x, 'ctx_1024': ctx_1024, 'L0_xattn_Wq': _L0_xattn_in['Wq'], 'L0_xattn_bq': _L0_xattn_in['bq'], 'L0_xattn_Wk': _L0_xattn_in['Wk'], 'L0_xattn_bk': _L0_xattn_in['bk'], 'L0_xattn_Wv': _L0_xattn_in['Wv'], 'L0_xattn_bv': _L0_xattn_in['bv'], 'L0_ffn_w1': _L0_ffn_in['w1'], 'L0_ffn_w2': _L0_ffn_in['w2'], 'L0_ffn_router_w': _L0_ffn_in['router_w']}

def reference(x, ctx_1024, L0_xattn_Wq, L0_xattn_bq, L0_xattn_Wk, L0_xattn_bk, L0_xattn_Wv, L0_xattn_bv, L0_ffn_w1, L0_ffn_w2, L0_ffn_router_w):
    import jax
    import jax.numpy as jnp

    def _L0_xattn_ref(query, key, value, Wq, bq, Wk, bk, Wv, bv):
        import jax, jax.numpy as jnp
        import numpy as np
        D = 128
        q = jnp.einsum('bnd,ed->bne', query, Wq) + bq
        k = jnp.einsum('bnd,ed->bne', key, Wk) + bk
        v = jnp.einsum('bnd,ed->bne', value, Wv) + bv
        scores = jnp.einsum('bqd,bkd->bqk', q, k)
        attn = jax.nn.softmax(scores, axis=-1)
        return jnp.einsum('bqk,bkd->bqd', attn, v)

    def _L0_ffn_ref(hidden_states, w1, w2, router_w):
        import jax, jax.numpy as jnp
        import numpy as np
        HIDDEN = 128
        INTER = 256
        NUM_EXPERTS = 8
        TOPK = 2
        STD = 0.02
        orig_shape = hidden_states.shape
        dtype = hidden_states.dtype
        x = hidden_states.reshape(-1, orig_shape[-1])
        E = w1.shape[0]
        gating = x @ router_w.T
        probs = jax.nn.softmax(gating.astype(jnp.float32), axis=-1)
        topk_w, sel = jax.lax.top_k(probs, TOPK)
        topk_w = topk_w.astype(dtype)
        combine = (jax.nn.one_hot(sel, E, dtype=dtype) * topk_w[..., None]).sum(axis=1)
        h = jnp.einsum('td,eid->tei', x, w1)
        gate = jax.nn.silu(h[..., :INTER])
        y = h[..., INTER:] * gate
        out = jnp.einsum('tei,ehi,te->th', y, w2, combine)
        return out.reshape(orig_shape)
    x = x + _L0_xattn_ref(_layernorm(x, axis=-1), ctx_1024, ctx_1024, L0_xattn_Wq, L0_xattn_bq, L0_xattn_Wk, L0_xattn_bk, L0_xattn_Wv, L0_xattn_bv)
    x = x + _L0_ffn_ref(_layernorm(x, axis=-1), L0_ffn_w1, L0_ffn_w2, L0_ffn_router_w)
    return x

_drawn_inputs = setup_inputs


def setup_inputs(seed=0):
    import zlib

    import numpy as np

    out = dict(_drawn_inputs(seed))
    spreads = {}
    factors = {'L0_xattn_bk': 8.0, 'L0_ffn_w1': 8.0, 'L0_ffn_w2': 8.0, 'L0_ffn_router_w': 8.0}
    for name, (base, spread) in spreads.items():
        noise = np.random.default_rng([zlib.crc32(name.encode()), seed]).standard_normal(out[name].shape)
        drawn = base * np.exp(spread * noise) if base else spread * noise
        out[name] = jnp.asarray(drawn.astype(out[name].dtype))
    for name, factor in factors.items():
        out[name] = (out[name] * factor).astype(out[name].dtype)
    return out
```

```python
import concourse.bass as bass
from concourse import mybir
from contextlib import ExitStack


def xattn_moe_kernel(
    nc: bass.Bass,
    x_rows: bass.AP,
    x_cols: bass.AP,
    key_pack: bass.AP,
    proj_pack: bass.AP,
    bv_row: bass.AP,
    w1_cols: bass.AP,
    w2_cols: bass.AP,
    out: bass.AP,
):
    fp32 = mybir.dt.float32
    fp32r = mybir.dt.float32r
    ALU = mybir.AluOpType
    ACT = mybir.ActivationFunctionType
    AX = mybir.AxisListType

    P = 128
    D = 128
    E = w2_cols.shape[1] // (2 * D)
    T = 512
    B = x_cols.shape[1] // T
    J = T // P
    KEYS = (key_pack.shape[1] - D - 2) // B
    S = 2 * E
    EPS = 1e-5
    FAR = 1e30

    BANKS = 2
    SIL = 4
    NY = 16
    NS = 4
    SPLIT_LAG = 10
    OUT_LAG = 12
    CPART = 4
    EP = E // CPART

    ctx = ExitStack()
    with ctx:
        def sb(name, shape, dt=fp32):
            return ctx.enter_context(nc.sbuf_tensor(name, shape, dt))

        def sem(name):
            return ctx.enter_context(nc.semaphore(name))

        x = sb("x", [P, B * J, D])
        xT = sb("xT", [D, B, T])
        kpack = sb("kpack", [D, B * KEYS + D + 2])
        ppack = sb("ppack", [D, 2 * D + E])
        bv = sb("bv", [KEYS, D])
        ctxT = kpack[:, 0:B * KEYS]
        wkT = kpack[:, B * KEYS:B * KEYS + D]
        bk = kpack[:, B * KEYS + D:B * KEYS + D + 1]
        bq = kpack[:, B * KEYS + D + 1:B * KEYS + D + 2]
        wq = ppack[:, 0:D]
        wvT = ppack[:, D:2 * D]
        wrT = ppack[:, 2 * D:2 * D + E]

        ident = sb("ident", [P, P])
        ones = sb("ones", [P, P])
        half_neg = sb("half_neg", [P, J])
        order = sb("order", [P, J, E])
        act_warm = sb("act_warm", [P, 1])

        wq_mean = sb("wq_mean", [D, 1])
        wq_scaled = sb("wq_scaled", [D, D])
        wq_c = sb("wq_c", [D, D])
        bq_rep = sb("bq_rep", [D, P])
        kT = sb("kT", [D, B * KEYS])
        mT = sb("mT", [D, B * KEYS])
        cbias = sb("cbias", [P, B * KEYS])
        v = sb("v", [KEYS, B, D])

        st = sb("st", [P, B * J, 6])
        mv = sb("mv", [P, B * J, 2])
        veps = sb("veps", [P, B * J])
        rstd = sb("rstd", [P, B * J])
        attn = sb("attn", [P, B * J, KEYS])
        nmax = sb("nmax", [P, B * J])
        esum = sb("esum", [P, B * J])
        rsum = sb("rsum", [P, B * J])
        eT = sb("eT", [KEYS, T])
        x2 = sb("x2", [P, J, D])
        st2 = sb("st2", [P, J, 6])
        mv2 = sb("mv2", [P, J, 2])
        veps2 = sb("veps2", [P, J])
        rstd2 = sb("rstd2", [P, J])
        xn2 = sb("xn2", [P, J, D])
        x2T = sb("x2T", [D, B, T])
        xh = sb("xh", [D, 2, T], fp32r)
        xl = sb("xl", [D, 2, T], fp32r)

        wr = sb("wr", [D, 2, E], fp32r)
        w1_hi = sb("w1_hi", [D, E, 4 * P], fp32r)
        w1_lo = sb("w1_lo", [D, E, 4 * P], fp32r)
        w2_hi = sb("w2_hi", [P, E, 2 * D], fp32r)
        w2_lo = sb("w2_lo", [P, E, 2 * D], fp32r)
        w2_raw = sb("w2_raw", [P, E, 2 * D])
        gates = sb("gates", [P, E, T])
        w1_raw = gates[:]

        top = sb("top", [P, J])
        top2 = sb("top2", [P, J])
        first1 = sb("first1", [P, J])
        first2 = sb("first2", [P, J])
        logits = sb("logits", [P, J, E])
        dist = sb("dist", [P, J, E])
        rest = sb("rest", [P, J, E])
        rest0 = sb("rest0", [P, J, E])
        mark1 = sb("mark1", [P, J, E])
        mark2 = sb("mark2", [P, J, E])
        pick1 = sb("pick1", [P, J, E])
        pick2 = sb("pick2", [P, J, E])
        picks = sb("picks", [P, J, E])
        tanh_h = sb("tanh_h", [P, J, E])
        den = sb("den", [P, J, E])
        rden = sb("rden", [P, J, E])
        prob = sb("prob", [P, J, E])
        psum_e = sb("psum_e", [P, J])
        rpsum = sb("rpsum", [P, J])
        probn = sb("probn", [P, J, E])
        comb = sb("comb", [P, E, J])
        combT = sb("combT", [E * J, P])

        silu = sb("silu", [P, SIL, T])
        y = sb("y", [P, NY, T])
        y_hi = sb("y_hi", [P, NS, T], fp32r)
        y_lo = sb("y_lo", [P, NS, T], fp32r)
        out_sb = sb("out_sb", [D, 2, T])

        comb_dram = nc.dram_tensor("comb_scratch", (B, E * J, P), fp32).ap()

        bank = [ctx.enter_context(nc.psum_tensor(f"bank{i}", [P, T], fp32)) for i in range(8)]
        gate_ps = bank[0:2]
        up_ps = bank[2:4]
        out_ps = bank[4]
        bank_e, bank_o, bank_r = bank[5], bank[6], bank[7]
        kT_ps, v_ps, m_ps, cb_ps = bank[0], bank[1], bank[2], bank[3]
        scores_ps = [bank_e, bank_o, bank_r, out_ps]

        s_kpack, s_ppack, s_bv = sem("s_kpack"), sem("s_ppack"), sem("s_bv")
        s_rows = [sem(f"s_rows{b}") for b in range(B)]
        s_cols = [sem(f"s_cols{b}") for b in range(B)]
        s_w1 = [sem(f"s_w1_{e}") for e in range(E)]
        s_w2 = [sem(f"s_w2_{e}") for e in range(2)]
        s_ident0, s_ident, s_ones, s_half, s_order = (
            sem("s_ident0"), sem("s_ident"), sem("s_ones"), sem("s_half"), sem("s_order"))
        s_wqmean, s_wqc, s_bqrep = sem("s_wqmean"), sem("s_wqc"), sem("s_bqrep")
        s_kT_ps, s_kT = sem("s_kT_ps"), sem("s_kT")
        s_v_ps, s_v = sem("s_v_ps"), sem("s_v")
        s_m_ps, s_mT = sem("s_m_ps"), sem("s_mT")
        s_cb_ps, s_cbias = sem("s_cb_ps"), sem("s_cbias")
        s_wrhi, s_wrlo = sem("s_wrhi"), sem("s_wrlo")
        s_w1hi, s_w1lo, s_w2hi, s_w2lo = sem("s_w1hi"), sem("s_w1lo"), sem("s_w2hi"), sem("s_w2lo")
        s_st, s_mv, s_veps, s_rstd = sem("s_st"), sem("s_mv"), sem("s_veps"), sem("s_rstd")
        s_score_ps, s_score, s_nmax, s_exp, s_rsum = (
            sem("s_score_ps"), sem("s_score"), sem("s_nmax"), sem("s_exp"), sem("s_rsum"))
        s_eT_ps, s_eT, s_av = sem("s_eT_ps"), sem("s_eT"), sem("s_av")
        s_x2, s_st2, s_mv2, s_veps2, s_rstd2, s_xn2 = (
            sem("s_x2"), sem("s_st2"), sem("s_mv2"), sem("s_veps2"), sem("s_rstd2"), sem("s_xn2"))
        s_x2T_ps, s_x2T, s_xnT_ps, s_xh, s_xl = (
            sem("s_x2T_ps"), sem("s_x2T"), sem("s_xnT_ps"), sem("s_xh"), sem("s_xl"))
        s_logit_ps, s_logits, s_top, s_dist, s_tanh = sem("s_logit_ps"), sem("s_logits"), sem("s_top"), sem("s_dist"), sem("s_tanh")
        s_mark1, s_first1, s_pick1, s_rest0, s_top2, s_rest, s_mark2, s_first2, s_pick2, s_picks = (
            sem("s_mark1"), sem("s_first1"), sem("s_pick1"), sem("s_rest0"), sem("s_top2"), sem("s_rest"),
            sem("s_mark2"), sem("s_first2"), sem("s_pick2"), sem("s_picks"))
        s_den, s_rden, s_prob, s_psum, s_rpsum, s_probn = (
            sem("s_den"), sem("s_rden"), sem("s_prob"), sem("s_psum"), sem("s_rpsum"), sem("s_probn"))
        s_comb, s_combT_ps, s_combT, s_comb_out = (
            sem("s_comb"), sem("s_combT_ps"), sem("s_combT"), sem("s_comb_out"))
        s_gates = [sem(f"s_gates{c}") for c in range(CPART)]
        s_gate, s_up, s_silu, s_y, s_yc, s_yh, s_yl, s_down = (
            sem("s_gate"), sem("s_up"), sem("s_silu"), sem("s_y"), sem("s_yc"), sem("s_yh"), sem("s_yl"),
            sem("s_down"))
        s_final, s_out = sem("s_final"), sem("s_out")

        block = ctx.enter_context(nc.Block())
        KEY_PARTS = [(0, KEYS), (KEYS, B * KEYS)]

        def bcast(ap, n):
            return ap.unsqueeze(2).to_broadcast([P, J, n])

        @block.sync
        def _(sp):
            sp.dma_start(kpack[:], key_pack).then_inc(s_kpack, 16)
            sp.dma_start(xT[:, 0, :], x_cols[:, 0:T]).then_inc(s_cols[0], 16)
            sp.dma_start(bv[:], bv_row.to_broadcast([KEYS, D])).then_inc(s_bv, 16)

            def load_w1(e):
                sp.dma_start(w1_raw[:, e, :], w1_cols[:, e * 4 * P:(e + 1) * 4 * P]).then_inc(s_w1[e], 16)

            def load_w2(part):
                half = E // 2
                sp.dma_start(w2_raw[:, part * half:(part + 1) * half, :],
                             w2_cols[:, part * half * 2 * D:(part + 1) * half * 2 * D]).then_inc(s_w2[part], 16)

            def store(b):
                sp.wait_ge(s_final, b + 1)
                sp.dma_start(out[:, b * T:(b + 1) * T], out_sb[:, b % 2, :]).then_inc(s_out, 16)

            load_w1(0)
            for b in range(1, B):
                sp.dma_start(x[:, b * J:(b + 1) * J, :],
                             x_rows[:, b * J * D:(b + 1) * J * D]).then_inc(s_rows[b], 16)
                sp.dma_start(xT[:, b, :], x_cols[:, b * T:(b + 1) * T]).then_inc(s_cols[b], 16)
            load_w1(1)
            load_w2(0)
            for e in range(2, E):
                load_w1(e)
            load_w2(1)

            for b in range(B):
                sp.wait_ge(s_combT, b + 1)
                sp.dma_start(comb_dram[b, :, :], combT[:]).then_inc(s_comb_out, 16)
                sp.wait_ge(s_comb_out, 16 * (b + 1))
                if b >= 1:
                    sp.wait_ge(s_yc, S * b)
                else:
                    sp.wait_ge(s_w1lo, E)
                for c in range(CPART):
                    src = comb_dram[b, c * EP * J:(c + 1) * EP * J, :].rearrange("r p -> (r p)")
                    sp.dma_start(gates[:, c * EP:(c + 1) * EP, :].rearrange("p e t -> p (e t)"),
                                 src.unsqueeze(0).to_broadcast([P, EP * T])).then_inc(s_gates[c], 16)
                if b >= 1:
                    store(b - 1)
            store(B - 1)
            sp.wait_ge(s_out, 16 * B)

        @block.gpsimd
        def _(pool):
            nc.gpsimd.memset(ident[:], 0.0).then_inc(s_ident0, 1)
            nc.gpsimd.memset(half_neg[:], -0.5).then_inc(s_half, 1)
            pool.wait_ge(s_ident0, 1)
            nc.gpsimd.affine_select(out=ident[:], in_=ident[:], compare_op=ALU.not_equal, fill=1.0, base=0,
                                    pattern=[[-1, P]], channel_multiplier=1).then_inc(s_ident, 1)

            pool.wait_ge(s_half, 1)

            def inverse_std(mean_var, v_eps, r_std, s_in, n_in, s_mid, s_done, n):
                pool.wait_ge(s_in, n_in)
                nc.gpsimd.tensor_scalar(v_eps, mean_var, EPS, None, ALU.add).then_inc(s_mid, 1)
                pool.wait_ge(s_mid, n)
                nc.gpsimd.tensor_tensor(r_std, v_eps, half_neg[:], ALU.pow).then_inc(s_done, 1)

            def first_norm(b):
                r = slice(b * J, (b + 1) * J)
                inverse_std(mv[:, r, 1], veps[:, r], rstd[:, r], s_mv, J * (b + 1), s_veps, s_rstd, b + 1)

            def second_norm(b):
                if b >= 1:
                    pool.wait_ge(s_xn2, J * b)
                inverse_std(mv2[:, :, 1], veps2[:], rstd2[:], s_mv2, J * (b + 1), s_veps2, s_rstd2, b + 1)

            def split_w1(e):
                pool.wait_ge(s_w1[e], 16)
                pool.wait_ge(s_w1hi, e + 1)
                nc.gpsimd.tensor_tensor(w1_lo[:, e, :], w1_raw[:, e, :], w1_hi[:, e, :].bitcast(fp32),
                                        ALU.subtract).then_inc(s_w1lo, 1)

            def split_w2(e):
                pool.wait_ge(s_w2[e // (E // 2)], 16)
                pool.wait_ge(s_w2hi, e + 1)
                nc.gpsimd.tensor_tensor(w2_lo[:, e, :], w2_raw[:, e, :], w2_hi[:, e, :].bitcast(fp32),
                                        ALU.subtract).then_inc(s_w2lo, 1)

            first_norm(0)
            split_w1(0)
            first_norm(1)
            second_norm(0)
            for b in range(2, B):
                first_norm(b)
            for e in range(1, E):
                split_w1(e)
                split_w2(e - 1)
            split_w2(E - 1)

            for b in range(B):
                if b + 1 < B:
                    second_norm(b + 1)
                for s in range(S):
                    g = S * b + s
                    if s % (S // CPART) == 0:
                        pool.wait_ge(s_gates[s // (S // CPART)], 16 * (b + 1))
                    pool.wait_ge(s_y, g + 1)
                    nc.gpsimd.tensor_tensor(y[:, g % NY, :], y[:, g % NY, :], gates[:, s // 2, :],
                                            ALU.mult).then_inc(s_yc, 1)

        @block.scalar
        def _(act):
            act.dma_start(ppack[:], proj_pack).then_inc(s_ppack, 16)
            act.dma_start(x[:, 0:J, :], x_rows[:, 0:J * D]).then_inc(s_rows[0], 16)
            act.wait_ge(s_ones, 1)
            nc.scalar.activation(act_warm[:], ones[:, 0:1], ACT.Exp)

            for i, (a, z) in enumerate(KEY_PARTS):
                act.wait_ge(s_kT_ps, i + 1)
                nc.scalar.activation(kT[:, a:z], kT_ps[:, a:z], ACT.Identity, bias=bk).then_inc(s_kT, 1)

            def softmax_exp(b):
                act.wait_ge(s_nmax, b + 1)
                for j in range(b * J, (b + 1) * J):
                    nc.scalar.activation(attn[:, j, :], attn[:, j, :], ACT.Exp, bias=nmax[:, j:j + 1],
                                         accum_out=esum[:, j:j + 1]).then_inc(s_exp, 1)

            def weights_hi(e):
                act.wait_ge(s_w1[e], 16)
                nc.scalar.activation(w1_hi[:, e, :], w1_raw[:, e, :], ACT.Copy).then_inc(s_w1hi, 1)
                act.wait_ge(s_w2[e // (E // 2)], 16)
                nc.scalar.activation(w2_hi[:, e, :], w2_raw[:, e, :], ACT.Copy).then_inc(s_w2hi, 1)

            def move_eT(b):
                act.wait_ge(s_eT_ps, b + 1)
                if b >= 1:
                    act.wait_ge(s_av, b)
                nc.scalar.activation(eT[:], bank_e[0:KEYS, :], ACT.Copy).then_inc(s_eT, 1)

            def move_x2T(b):
                act.wait_ge(s_x2T_ps, b + 1)
                nc.scalar.activation(x2T[:, b, :], bank_o[:], ACT.Copy).then_inc(s_x2T, 1)

            def round_x(b):
                act.wait_ge(s_xnT_ps, b + 1)
                nc.scalar.activation(xh[:, b % 2, :], bank_e[:], ACT.Copy).then_inc(s_xh, 1)

            def router_tanh(b):
                act.wait_ge(s_dist, b + 1)
                if b >= 1:
                    act.wait_ge(s_prob, b)
                nc.scalar.activation(tanh_h[:], dist[:], ACT.Tanh, scale=0.5).then_inc(s_tanh, 1)

            def move_combT(b):
                act.wait_ge(s_combT_ps, b + 1)
                if b >= 1:
                    act.wait_ge(s_comb_out, 16 * b)
                nc.scalar.activation(combT[:], bank_r[0:E * J, 0:P], ACT.Copy).then_inc(s_combT, 1)

            def silu_step(g):
                act.wait_ge(s_gate, g + 1)
                if g >= SIL:
                    act.wait_ge(s_y, g - SIL + 1)
                nc.scalar.activation(silu[:, g % SIL, :], gate_ps[g % 2][:], ACT.Silu).then_inc(s_silu, 1)

            def round_y(g):
                act.wait_ge(s_yc, g + 1)
                if g >= NS:
                    act.wait_ge(s_down, g - NS + 1)
                nc.scalar.activation(y_hi[:, g % NS, :], y[:, g % NY, :], ACT.Copy).then_inc(s_yh, 1)

            softmax_exp(0)
            move_eT(0)
            weights_hi(0)
            softmax_exp(1)
            move_x2T(0)
            weights_hi(1)
            weights_hi(2)
            round_x(0)
            for b in range(2, B):
                softmax_exp(b)
            router_tanh(0)

            for b in range(B):
                for s in range(S):
                    g = S * b + s
                    silu_step(g)
                    if b == 0 and s < E - 3:
                        weights_hi(s + 3)
                    if g >= SPLIT_LAG:
                        round_y(g - SPLIT_LAG)
                    if s == 4:
                        move_combT(b)
                    if b + 1 < B:
                        if s == 1:
                            move_eT(b + 1)
                        if s == 6:
                            move_x2T(b + 1)
                        if s == 9:
                            round_x(b + 1)
                        if s == 12:
                            router_tanh(b + 1)
            for g in range(S * B - SPLIT_LAG, S * B):
                round_y(g)

        @block.vector
        def _(dve):
            nc.vector.memset(ones[:], 1.0).then_inc(s_ones, 1)
            for e in range(E):
                last = nc.vector.memset(order[:, :, e], float(E - e))
            last.then_inc(s_order, 1)

            def first_stats(b):
                dve.wait_ge(s_rows[b], 16)
                for j in range(b * J, (b + 1) * J):
                    nc.vector.bn_stats(st[:, j, :], x[:, j, :]).then_inc(s_st, 1)
                for j in range(b * J, (b + 1) * J):
                    dve.wait_ge(s_st, j + 1)
                    nc.vector.bn_aggr(mv[:, j, :], st[:, j, :]).then_inc(s_mv, 1)

            def centre_wq():
                dve.wait_ge(s_ppack, 16)
                nc.vector.tensor_scalar(wq_scaled[:], wq, 1.0 / D, None, ALU.mult, ALU.add,
                                        accum_out=wq_mean[:]).then_inc(s_wqmean, 1)
                dve.wait_ge(s_kpack, 16)
                dve.wait_ge(s_ones, 1)
                nc.vector.tensor_scalar(bq_rep[:], ones[:], bq, None, ALU.mult).then_inc(s_bqrep, 1)
                dve.wait_ge(s_wqmean, 1)
                nc.vector.tensor_scalar(wq_c[:], wq, wq_mean[:], None, ALU.subtract).then_inc(s_wqc, 1)

            def split_router():
                nc.vector.tensor_copy(wr[:, 0, :], wrT).then_inc(s_wrhi, 1)
                dve.wait_ge(s_wrhi, 1)
                nc.vector.tensor_tensor(wr[:, 1, :], wrT, wr[:, 0, :].bitcast(fp32), ALU.subtract).then_inc(s_wrlo, 1)

            def move_keys(i):
                a, z = KEY_PARTS[i]
                dve.wait_ge(s_m_ps, i + 1)
                nc.vector.tensor_copy(mT[:, a:z], m_ps[:, a:z]).then_inc(s_mT, 1)
                dve.wait_ge(s_cb_ps, i + 1)
                nc.vector.tensor_copy(cbias[:, a:z], cb_ps[:, a:z]).then_inc(s_cbias, 1)

            def move_v():
                dve.wait_ge(s_v_ps, 1)
                dve.wait_ge(s_bv, 16)
                nc.vector.tensor_tensor(v[:], v_ps[0:KEYS, :].rearrange("k (b d) -> k b d", d=D),
                                        bv[:].unsqueeze(1).to_broadcast([KEYS, B, D]), ALU.add).then_inc(s_v, 1)

            def scale_scores(b):
                dve.wait_ge(s_score_ps, b + 1)
                dve.wait_ge(s_rstd, b + 1)
                dve.wait_ge(s_cbias, 1 if b == 0 else 2)
                for j in range(J):
                    n = b * J + j
                    nc.vector.scalar_tensor_tensor(
                        out=attn[:, n, :], in0=scores_ps[b][:, j * KEYS:(j + 1) * KEYS], scalar=rstd[:, n:n + 1],
                        in1=cbias[:, b * KEYS:(b + 1) * KEYS], op0=ALU.mult, op1=ALU.add).then_inc(s_score, 1)
                dve.wait_ge(s_score, J * (b + 1))
                nc.vector.tensor_reduce(nmax[:, b * J:(b + 1) * J], attn[:, b * J:(b + 1) * J, :], AX.X, ALU.max,
                                        negate=True).then_inc(s_nmax, 1)

            def invert_sum(b):
                dve.wait_ge(s_exp, J * (b + 1))
                nc.vector.reciprocal(rsum[:, b * J:(b + 1) * J], esum[:, b * J:(b + 1) * J]).then_inc(s_rsum, 1)

            def attend(b, tiles):
                dve.wait_ge(s_av, b + 1)
                dve.wait_ge(s_rsum, b + 1)
                if b >= 1:
                    dve.wait_ge(s_x2T_ps, b)
                for j in tiles:
                    n = b * J + j
                    nc.vector.scalar_tensor_tensor(
                        out=x2[:, j, :], in0=bank_o[:, j * D:(j + 1) * D], scalar=rsum[:, n:n + 1],
                        in1=x[:, n, :], op0=ALU.mult, op1=ALU.add).then_inc(s_x2, 1)

            def second_stats(b, tiles):
                for j in tiles:
                    dve.wait_ge(s_x2, J * b + j + 1)
                    nc.vector.bn_stats(st2[:, j, :], x2[:, j, :]).then_inc(s_st2, 1)

            def second_moments(b):
                if b >= 1:
                    dve.wait_ge(s_veps2, b)
                for j in range(J):
                    dve.wait_ge(s_st2, J * b + j + 1)
                    nc.vector.bn_aggr(mv2[:, j, :], st2[:, j, :]).then_inc(s_mv2, 1)

            def normalise(b, tiles):
                dve.wait_ge(s_rstd2, b + 1)
                if b >= 1:
                    dve.wait_ge(s_xnT_ps, b)
                for j in tiles:
                    nc.vector.tensor_scalar(xn2[:, j, :], x2[:, j, :], mv2[:, j, 0:1], rstd2[:, j:j + 1],
                                            ALU.subtract, ALU.mult).then_inc(s_xn2, 1)

            def split_x(b):
                dve.wait_ge(s_xh, b + 1)
                nc.vector.tensor_tensor(xl[:, b % 2, :], bank_e[:], xh[:, b % 2, :].bitcast(fp32),
                                        ALU.subtract).then_inc(s_xl, 1)

            logit_parts = bank_r[:, 0:J * 2 * E].rearrange("p (j h e) -> p j e h", h=2, e=E)

            def r_logits(b):
                dve.wait_ge(s_logit_ps, b + 1)
                nc.vector.tensor_reduce(logits[:], logit_parts, AX.X, ALU.add).then_inc(s_logits, 1)

            def r_top(b):
                dve.wait_ge(s_logits, b + 1)
                nc.vector.tensor_reduce(top[:], logits[:], AX.X, ALU.max).then_inc(s_top, 1)

            def r_dist(b):
                dve.wait_ge(s_top, b + 1)
                nc.vector.tensor_tensor(dist[:], logits[:], bcast(top[:], E), ALU.subtract).then_inc(s_dist, 1)

            def r_mark1(b):
                dve.wait_ge(s_dist, b + 1)
                nc.vector.scalar_tensor_tensor(out=mark1[:], in0=dist[:], scalar=0.0, in1=order[:],
                                               op0=ALU.is_equal, op1=ALU.mult).then_inc(s_mark1, 1)

            def r_first1(b):
                dve.wait_ge(s_mark1, b + 1)
                nc.vector.tensor_reduce(first1[:], mark1[:], AX.X, ALU.max).then_inc(s_first1, 1)

            def r_pick1(b):
                dve.wait_ge(s_first1, b + 1)
                nc.vector.tensor_tensor(pick1[:], mark1[:], bcast(first1[:], E), ALU.is_equal).then_inc(s_pick1, 1)

            def r_rest0(b):
                dve.wait_ge(s_pick1, b + 1)
                nc.vector.scalar_tensor_tensor(out=rest0[:], in0=pick1[:], scalar=-FAR, in1=dist[:],
                                               op0=ALU.mult, op1=ALU.add).then_inc(s_rest0, 1)

            def r_top2(b):
                dve.wait_ge(s_rest0, b + 1)
                nc.vector.tensor_reduce(top2[:], rest0[:], AX.X, ALU.max).then_inc(s_top2, 1)

            def r_rest(b):
                dve.wait_ge(s_top2, b + 1)
                nc.vector.tensor_tensor(rest[:], rest0[:], bcast(top2[:], E), ALU.is_equal).then_inc(s_rest, 1)

            def r_mark2(b):
                dve.wait_ge(s_rest, b + 1)
                nc.vector.tensor_tensor(mark2[:], rest[:], order[:], ALU.mult).then_inc(s_mark2, 1)

            def r_first2(b):
                dve.wait_ge(s_mark2, b + 1)
                nc.vector.tensor_reduce(first2[:], mark2[:], AX.X, ALU.max).then_inc(s_first2, 1)

            def r_pick2(b):
                dve.wait_ge(s_first2, b + 1)
                nc.vector.tensor_tensor(pick2[:], mark2[:], bcast(first2[:], E), ALU.is_equal).then_inc(s_pick2, 1)

            def r_picks(b):
                dve.wait_ge(s_pick2, b + 1)
                nc.vector.tensor_tensor(picks[:], pick1[:], pick2[:], ALU.add).then_inc(s_picks, 1)

            def r_den(b):
                dve.wait_ge(s_tanh, b + 1)
                nc.vector.tensor_scalar(den[:], tanh_h[:], -1.0, 1.0, ALU.mult, ALU.add).then_inc(s_den, 1)

            def r_rden(b):
                dve.wait_ge(s_den, b + 1)
                nc.vector.reciprocal(rden[:], den[:]).then_inc(s_rden, 1)

            def r_prob(b):
                dve.wait_ge(s_rden, b + 1)
                nc.vector.scalar_tensor_tensor(out=prob[:], in0=tanh_h[:], scalar=1.0, in1=rden[:],
                                               op0=ALU.add, op1=ALU.mult).then_inc(s_prob, 1)

            def r_psum(b):
                dve.wait_ge(s_prob, b + 1)
                nc.vector.tensor_reduce(psum_e[:], prob[:], AX.X, ALU.add).then_inc(s_psum, 1)

            def r_rpsum(b):
                dve.wait_ge(s_psum, b + 1)
                nc.vector.reciprocal(rpsum[:], psum_e[:]).then_inc(s_rpsum, 1)

            def r_probn(b):
                dve.wait_ge(s_rpsum, b + 1)
                nc.vector.tensor_tensor(probn[:], prob[:], bcast(rpsum[:], E), ALU.mult).then_inc(s_probn, 1)

            def r_comb(b):
                dve.wait_ge(s_picks, b + 1)
                dve.wait_ge(s_probn, b + 1)
                if b >= 1:
                    dve.wait_ge(s_combT_ps, b)
                nc.vector.tensor_tensor(comb[:].rearrange("p e j -> p j e"), picks[:], probn[:],
                                        ALU.mult).then_inc(s_comb, 1)

            def multiply(g):
                dve.wait_ge(s_up, g + 1)
                dve.wait_ge(s_silu, g + 1)
                if g >= NY:
                    dve.wait_ge(s_yl, g - NY + 1)
                nc.vector.tensor_tensor(y[:, g % NY, :], up_ps[g % 2][:], silu[:, g % SIL, :],
                                        ALU.mult).then_inc(s_y, 1)

            def split_y(g):
                dve.wait_ge(s_yh, g + 1)
                if g >= NS:
                    dve.wait_ge(s_down, g - NS + 1)
                nc.vector.tensor_tensor(y_lo[:, g % NS, :], y[:, g % NY, :], y_hi[:, g % NS, :].bitcast(fp32),
                                        ALU.subtract).then_inc(s_yl, 1)

            def finish(b):
                dve.wait_ge(s_down, S * (b + 1))
                dve.wait_ge(s_x2T, b + 1)
                if b >= 2:
                    dve.wait_ge(s_out, 16 * (b - 1))
                nc.vector.tensor_tensor(out_sb[:, b % 2, :], out_ps[:], x2T[:, b, :], ALU.add).then_inc(s_final, 1)

            def router_slot(b, slot):
                if slot == 0:
                    r_logits(b)
                    r_top(b)
                    r_dist(b)
                if slot == 1:
                    r_mark1(b)
                    r_first1(b)
                if slot == 2:
                    r_pick1(b)
                    r_den(b)
                    r_rest0(b)
                    r_rden(b)
                if slot == 3:
                    r_top2(b)
                    r_prob(b)
                    r_rest(b)
                    r_psum(b)
                if slot == 4:
                    r_mark2(b)
                    r_rpsum(b)
                    r_first2(b)
                    r_probn(b)
                if slot == 5:
                    r_pick2(b)
                    r_picks(b)
                if slot == 6:
                    r_comb(b)

            centre_wq()
            first_stats(0)
            move_keys(0)
            first_stats(1)
            scale_scores(0)
            move_keys(1)
            scale_scores(1)
            move_v()
            invert_sum(0)
            attend(0, range(J))
            second_stats(0, range(J))
            second_moments(0)
            dve.wait_ge(s_order, 1)
            split_router()
            first_stats(2)
            normalise(0, range(J))
            first_stats(3)
            scale_scores(2)
            split_x(0)
            scale_scores(3)
            for b in range(1, B):
                invert_sum(b)
            for slot in range(7):
                router_slot(0, slot)

            for b in range(B):
                for s in range(S):
                    g = S * b + s
                    multiply(g)
                    if b + 1 < B:
                        if s == 4:
                            second_stats(b + 1, range(J))
                            second_moments(b + 1)
                        if s == 8:
                            normalise(b + 1, range(J))
                        if s >= 12:
                            router_slot(b + 1, 2 * (s - 12))
                    if g >= SPLIT_LAG:
                        split_y(g - SPLIT_LAG)
                    if b + 1 < B:
                        if s == 3:
                            attend(b + 1, range(J))
                        if s == 10:
                            split_x(b + 1)
                        if 12 <= s < 15:
                            router_slot(b + 1, 2 * (s - 12) + 1)
                    if b >= 1 and s == OUT_LAG - 1:
                        finish(b - 1)
            for g in range(S * B - SPLIT_LAG, S * B):
                split_y(g)
            finish(B - 1)

        @block.tensor
        def _(pe):
            def project_keys(i):
                a, z = KEY_PARTS[i]
                nc.tensor.matmul(kT_ps[:, a:z], wkT, ctxT[:, a:z], start=True, stop=True).then_inc(s_kT_ps, 1)

            def fold_query(i):
                a, z = KEY_PARTS[i]
                pe.wait_ge(s_kT, i + 1)
                if i >= 1:
                    pe.wait_ge(s_mT, i)
                    pe.wait_ge(s_cbias, i)
                nc.tensor.matmul(m_ps[:, a:z], wq_c[:], kT[:, a:z], start=True, stop=True).then_inc(s_m_ps, 1)
                nc.tensor.matmul(cb_ps[:, a:z], bq_rep[:], kT[:, a:z], start=True, stop=True).then_inc(s_cb_ps, 1)

            def project_values():
                for b in range(B):
                    last = nc.tensor.matmul(v_ps[0:KEYS, b * D:(b + 1) * D], ctxT[:, b * KEYS:(b + 1) * KEYS], wvT,
                                            start=True, stop=True)
                last.then_inc(s_v_ps, 1)

            def score(b):
                pe.wait_ge(s_cols[b], 16)
                pe.wait_ge(s_mT, 1 if b == 0 else 2)
                for j in range(J):
                    last = nc.tensor.matmul(scores_ps[b][:, j * KEYS:(j + 1) * KEYS], xT[:, b, j * P:(j + 1) * P],
                                            mT[:, b * KEYS:(b + 1) * KEYS], start=True, stop=True)
                last.then_inc(s_score_ps, 1)

            def transpose_attn(b):
                pe.wait_ge(s_exp, J * (b + 1))
                if b >= 1:
                    pe.wait_ge(s_xl, b)
                for j in range(J):
                    last = nc.tensor.transpose(bank_e[0:KEYS, j * P:(j + 1) * P], attn[:, b * J + j, :], ident[:])
                last.then_inc(s_eT_ps, 1)

            def weigh_values(b):
                pe.wait_ge(s_eT, b + 1)
                pe.wait_ge(s_v, 1)
                if b >= 1:
                    pe.wait_ge(s_x2T, b)
                else:
                    pe.wait_ge(s_score, 2 * J)
                for j in range(J):
                    last = nc.tensor.matmul(bank_o[:, j * D:(j + 1) * D], eT[:, j * P:(j + 1) * P], v[:, b, :],
                                            start=True, stop=True)
                last.then_inc(s_av, 1)

            def transpose_x2(b):
                pe.wait_ge(s_x2, J * (b + 1))
                for j in range(J):
                    last = nc.tensor.transpose(bank_o[:, j * P:(j + 1) * P], x2[:, j, :], ident[:])
                last.then_inc(s_x2T_ps, 1)

            def transpose_xn(b):
                pe.wait_ge(s_xn2, J * (b + 1))
                for j in range(J):
                    last = nc.tensor.transpose(bank_e[:, j * P:(j + 1) * P], xn2[:, j, :], ident[:])
                last.then_inc(s_xnT_ps, 1)

            def route(b):
                pe.wait_ge(s_xl, b + 1)
                pe.wait_ge(s_wrlo, 1)
                if b >= 1:
                    pe.wait_ge(s_combT, b)
                else:
                    pe.wait_ge(s_score, 3 * J)
                for j in range(J):
                    o = bank_r[:, j * 2 * E:(j + 1) * 2 * E]
                    t = slice(j * P, (j + 1) * P)
                    nc.tensor.matmul(o, xh[:, b % 2, t], wr[:].rearrange("d h e -> d (h e)"), start=True, stop=False)
                    last = nc.tensor.matmul(o[:, 0:E], xl[:, b % 2, t], wr[:, 0, :], start=False, stop=True)
                last.then_inc(s_logit_ps, 1)

            def transpose_comb(b):
                pe.wait_ge(s_comb, b + 1)
                nc.tensor.transpose(bank_r[0:E * J, 0:P], comb[:].rearrange("p e j -> p (e j)"),
                                    ident[:]).then_inc(s_combT_ps, 1)

            def expand(b, s):
                g = S * b + s
                e, h = s // 2, s % 2
                if s == 0:
                    pe.wait_ge(s_xl, b + 1)
                if b == 0:
                    pe.wait_ge(s_w1lo, e + 1)
                for o, at, free, done in ((gate_ps[g % 2], 2 * h, s_silu, s_gate), (up_ps[g % 2], 2 * h + 1, s_y, s_up)):
                    if g >= BANKS:
                        pe.wait_ge(free, g - BANKS + 1)
                    c = slice(at * P, (at + 1) * P)
                    nc.tensor.matmul(o[:], w1_hi[:, e, c], xh[:, b % 2, :], start=True, stop=False)
                    nc.tensor.matmul(o[:], w1_hi[:, e, c], xl[:, b % 2, :], start=False, stop=False)
                    nc.tensor.matmul(o[:], w1_lo[:, e, c], xh[:, b % 2, :], start=False, stop=True).then_inc(done, 1)

            def contract(g):
                b, s = g // S, g % S
                e, h = s // 2, s % 2
                pe.wait_ge(s_yl, g + 1)
                if b == 0:
                    pe.wait_ge(s_w2lo, e + 1)
                if s == 0:
                    if b >= 1:
                        pe.wait_ge(s_final, b)
                    else:
                        pe.wait_ge(s_score, 4 * J)
                c = slice(h * D, (h + 1) * D)
                nc.tensor.matmul(out_ps[:], w2_hi[:, e, c], y_hi[:, g % NS, :], start=s == 0, stop=False)
                nc.tensor.matmul(out_ps[:], w2_hi[:, e, c], y_lo[:, g % NS, :], start=False, stop=False)
                nc.tensor.matmul(out_ps[:], w2_lo[:, e, c], y_hi[:, g % NS, :], start=False,
                                 stop=s == S - 1).then_inc(s_down, 1)

            pe.wait_ge(s_kpack, 16)
            project_keys(0)
            pe.wait_ge(s_wqc, 1)
            fold_query(0)
            score(0)
            project_keys(1)
            fold_query(1)
            score(1)
            project_values()
            pe.wait_ge(s_ident, 1)
            transpose_attn(0)
            weigh_values(0)
            score(2)
            score(3)
            transpose_x2(0)
            transpose_xn(0)
            route(0)

            for b in range(B):
                for s in range(S):
                    g = S * b + s
                    expand(b, s)
                    if g >= OUT_LAG:
                        contract(g - OUT_LAG)
                    if s == 4:
                        transpose_comb(b)
                    if b + 1 < B:
                        if s == 1:
                            transpose_attn(b + 1)
                        if s == 3:
                            weigh_values(b + 1)
                        if s == 6:
                            transpose_x2(b + 1)
                        if s == 9:
                            transpose_xn(b + 1)
                        if s == 11:
                            route(b + 1)
            for g in range(S * B - OUT_LAG, S * B):
                contract(g)


def kernel(**inputs):
    import numpy as np
    import concourse.bacc as bacc
    from concourse.bass_utils import run_bass_kernel_spmd

    x = np.asarray(inputs["x"])
    context = np.asarray(inputs["ctx_1024"])
    B, T, D = x.shape
    w1 = np.asarray(inputs["L0_ffn_w1"])
    w2 = np.asarray(inputs["L0_ffn_w2"])
    E = w1.shape[0]
    P = 128
    tokens = x.reshape(B * T, D)
    arrays = {
        "x_rows": tokens.reshape(B * T // P, P, D).transpose(1, 0, 2).reshape(P, -1),
        "x_cols": tokens.T,
        "key_pack": np.concatenate([context.reshape(-1, D).T, np.asarray(inputs["L0_xattn_Wk"]).T,
                                    np.asarray(inputs["L0_xattn_bk"])[:, None],
                                    np.asarray(inputs["L0_xattn_bq"])[:, None]], axis=1),
        "proj_pack": np.concatenate([np.asarray(inputs["L0_xattn_Wq"]), np.asarray(inputs["L0_xattn_Wv"]).T,
                                     np.asarray(inputs["L0_ffn_router_w"]).T], axis=1),
        "bv_row": np.asarray(inputs["L0_xattn_bv"])[None, :],
        "w1_cols": w1.reshape(E, 2, 2, P, D).transpose(4, 0, 2, 1, 3).reshape(D, -1),
        "w2_cols": w2.reshape(E, D, 2, P).transpose(3, 0, 2, 1).reshape(P, -1),
    }
    arrays = {name: np.ascontiguousarray(a) for name, a in arrays.items()}

    nc = bacc.Bacc("TRN2", target_bir_lowering=False, num_devices=1)
    args = {name: nc.dram_tensor(name, a.shape, mybir.dt.from_np(a.dtype), kind="ExternalInput").ap()
            for name, a in arrays.items()}
    out = nc.dram_tensor("out", (D, B * T), mybir.dt.float32, kind="ExternalOutput").ap()
    xattn_moe_kernel(nc, out=out, **args)
    r = run_bass_kernel_spmd(nc, [arrays], core_ids=[0])
    return np.ascontiguousarray(r.results[0]["out"].T).reshape(B, T, D)
```

```python
import concourse.bass as bass
from concourse import mybir
from contextlib import ExitStack


def xattn_moe_kernel(
    nc: bass.Bass,
    x_rows: bass.AP,
    x_cols: bass.AP,
    first_pack: bass.AP,
    wq_rows: bass.AP,
    later_pack: bass.AP,
    bv_row: bass.AP,
    w1_cols: bass.AP,
    w2_cols: bass.AP,
    out: bass.AP,
):
    fp32 = mybir.dt.float32
    fp32r = mybir.dt.float32r
    ALU = mybir.AluOpType
    ACT = mybir.ActivationFunctionType
    AX = mybir.AxisListType

    P = 128
    D = 128
    E = w2_cols.shape[1] // (2 * D)
    T = 512
    B = x_cols.shape[1] // T
    J = T // P
    KEYS = first_pack.shape[1] - D - 2
    S = 2 * E
    EPS = 1e-5
    FAR = 1e30

    BANKS = 2
    SIL = 4
    NY = 16
    NS = 4
    SPLIT_LAG = 10
    OUT_LAG = 12
    CPART = 4
    EXP_AT = 14
    NORM_AT = 7
    FIRST_COMB_AT = 4
    COMB_AT = 1
    EP = E // CPART

    ctx = ExitStack()
    with ctx:
        def sb(name, shape, dt=fp32):
            return ctx.enter_context(nc.sbuf_tensor(name, shape, dt))

        def sem(name):
            return ctx.enter_context(nc.semaphore(name))

        x = sb("x", [P, B * J, D])
        xT = sb("xT", [D, B, T])
        fpack = sb("fpack", [D, KEYS + D + 2])
        wq = sb("wq", [D, D])
        lpack = sb("lpack", [D, (B - 1) * KEYS + D + E])
        bv = sb("bv", [KEYS, D])
        wkT = fpack[:, KEYS:KEYS + D]
        bk = fpack[:, KEYS + D:KEYS + D + 1]
        bq = fpack[:, KEYS + D + 1:KEYS + D + 2]
        wvT = lpack[:, (B - 1) * KEYS:(B - 1) * KEYS + D]
        wrT = lpack[:, (B - 1) * KEYS + D:(B - 1) * KEYS + D + E]

        def context(a, z):
            return fpack[:, a:z] if z <= KEYS else lpack[:, a - KEYS:z - KEYS]

        ident = sb("ident", [P, P])
        ones = sb("ones", [P, P])
        half_neg = sb("half_neg", [P, J])
        order = sb("order", [P, J, E])
        act_warm = sb("act_warm", [P, 1])

        wq_mean = sb("wq_mean", [D, 1])
        wq_scaled = sb("wq_scaled", [D, D])
        wq_c = sb("wq_c", [D, D])
        bq_rep = sb("bq_rep", [D, P])
        kT = sb("kT", [D, B * KEYS])
        mT = sb("mT", [D, B * KEYS])
        cbias = sb("cbias", [P, B * KEYS])
        v = sb("v", [KEYS, B, D])

        st = sb("st", [P, B * J, 6])
        mv = sb("mv", [P, B * J, 2])
        veps = sb("veps", [P, B * J])
        rstd = sb("rstd", [P, B * J])
        attn = sb("attn", [P, B * J, KEYS])
        nmax = sb("nmax", [P, B * J])
        esum = sb("esum", [P, B * J])
        rsum = sb("rsum", [P, B * J])
        eT = sb("eT", [KEYS, T])
        x2 = sb("x2", [P, J, D])
        st2 = sb("st2", [P, J, 6])
        mv2 = sb("mv2", [P, J, 2])
        veps2 = sb("veps2", [P, J])
        rstd2 = sb("rstd2", [P, J])
        xn2 = sb("xn2", [P, J, D])
        x2T = sb("x2T", [D, B, T])
        xh = sb("xh", [D, 2, T], fp32r)
        xl = sb("xl", [D, 2, T], fp32r)

        wr = sb("wr", [D, 2, E], fp32r)
        w1_hi = sb("w1_hi", [D, E, 4 * P], fp32r)
        w1_lo = sb("w1_lo", [D, E, 4 * P], fp32r)
        w2_hi = sb("w2_hi", [P, E, 2 * D], fp32r)
        w2_lo = sb("w2_lo", [P, E, 2 * D], fp32r)
        w2_raw = sb("w2_raw", [P, E, 2 * D])
        gates = sb("gates", [P, E, T])
        w1_raw = gates[:]

        top = sb("top", [P, J])
        top2 = sb("top2", [P, J])
        first1 = sb("first1", [P, J])
        first2 = sb("first2", [P, J])
        logits = sb("logits", [P, J, E])
        dist = sb("dist", [P, J, E])
        rest = sb("rest", [P, J, E])
        rest0 = sb("rest0", [P, J, E])
        mark1 = sb("mark1", [P, J, E])
        mark2 = sb("mark2", [P, J, E])
        pick1 = sb("pick1", [P, J, E])
        pick2 = sb("pick2", [P, J, E])
        picks = sb("picks", [P, J, E])
        tanh_h = sb("tanh_h", [P, J, E])
        den = sb("den", [P, J, E])
        rden = sb("rden", [P, J, E])
        prob = sb("prob", [P, J, E])
        psum_e = sb("psum_e", [P, J])
        rpsum = sb("rpsum", [P, J])
        probn = sb("probn", [P, J, E])
        comb = sb("comb", [P, E, J])
        combT = sb("combT", [E * J, P])

        silu = sb("silu", [P, SIL, T])
        y = sb("y", [P, NY, T])
        y_hi = sb("y_hi", [P, NS, T], fp32r)
        y_lo = sb("y_lo", [P, NS, T], fp32r)
        out_sb = sb("out_sb", [D, 2, T])

        comb_dram = nc.dram_tensor("comb_scratch", (B, E * J, P), fp32).ap()

        bank = [ctx.enter_context(nc.psum_tensor(f"bank{i}", [P, T], fp32)) for i in range(8)]
        gate_ps = bank[0:2]
        up_ps = bank[2:4]
        out_ps = bank[4]
        bank_e, bank_o, bank_r = bank[5], bank[6], bank[7]
        kT_ps, v_ps, m_ps, cb_ps = bank[0], bank[1], bank[2], bank[3]
        scores_ps = [bank_e, out_ps, bank[3], bank[1]]

        def parts(b):
            return [range(0, J // 2), range(J // 2, J)] if b == 0 else [range(J)]

        def attn_bank(b, j):
            return bank_r if b == 0 and j >= J // 2 else bank_e

        def value_bank(b, j):
            return bank[1] if b == 0 and j >= J // 2 else bank_o

        s_fpack, s_wq, s_lpack, s_bv = sem("s_fpack"), sem("s_wq"), sem("s_lpack"), sem("s_bv")
        s_rows = [sem(f"s_rows{b}") for b in range(B)]
        s_cols = [sem(f"s_cols{b}") for b in range(B)]
        s_w1 = [sem(f"s_w1_{e}") for e in range(E)]
        s_w2 = [sem(f"s_w2_{e}") for e in range(2)]
        s_ident0, s_ident, s_ones, s_half, s_order = (
            sem("s_ident0"), sem("s_ident"), sem("s_ones"), sem("s_half"), sem("s_order"))
        s_wqmean, s_wqc, s_bqrep = sem("s_wqmean"), sem("s_wqc"), sem("s_bqrep")
        s_kT_ps, s_kT = sem("s_kT_ps"), sem("s_kT")
        s_v_ps, s_v = sem("s_v_ps"), sem("s_v")
        s_m_ps, s_mT = sem("s_m_ps"), sem("s_mT")
        s_cb_ps, s_cbias = sem("s_cb_ps"), sem("s_cbias")
        s_wrhi, s_wrlo = sem("s_wrhi"), sem("s_wrlo")
        s_w1hi, s_w1lo, s_w2hi, s_w2lo = sem("s_w1hi"), sem("s_w1lo"), sem("s_w2hi"), sem("s_w2lo")
        s_st, s_mv, s_veps, s_rstd = sem("s_st"), sem("s_mv"), sem("s_veps"), sem("s_rstd")
        s_score_ps, s_score, s_nmax, s_exp, s_rsum = (
            sem("s_score_ps"), sem("s_score"), sem("s_nmax"), sem("s_exp"), sem("s_rsum"))
        s_scaled, s_shift, s_esum = sem("s_scaled"), sem("s_shift"), sem("s_esum")
        s_eT_ps, s_eT, s_av = sem("s_eT_ps"), sem("s_eT"), sem("s_av")
        s_x2, s_st2, s_mv2, s_veps2, s_rstd2, s_xn2 = (
            sem("s_x2"), sem("s_st2"), sem("s_mv2"), sem("s_veps2"), sem("s_rstd2"), sem("s_xn2"))
        s_x2T_ps, s_x2T, s_xnT_ps, s_xh, s_xl = (
            sem("s_x2T_ps"), sem("s_x2T"), sem("s_xnT_ps"), sem("s_xh"), sem("s_xl"))
        s_logit_ps, s_logits, s_top, s_dist, s_tanh = sem("s_logit_ps"), sem("s_logits"), sem("s_top"), sem("s_dist"), sem("s_tanh")
        s_mark1, s_first1, s_pick1, s_rest0, s_top2, s_rest, s_mark2, s_first2, s_pick2, s_picks = (
            sem("s_mark1"), sem("s_first1"), sem("s_pick1"), sem("s_rest0"), sem("s_top2"), sem("s_rest"),
            sem("s_mark2"), sem("s_first2"), sem("s_pick2"), sem("s_picks"))
        s_den, s_rden, s_prob, s_psum, s_rpsum, s_probn = (
            sem("s_den"), sem("s_rden"), sem("s_prob"), sem("s_psum"), sem("s_rpsum"), sem("s_probn"))
        s_comb, s_combT_ps, s_combT, s_comb_out = (
            sem("s_comb"), sem("s_combT_ps"), sem("s_combT"), sem("s_comb_out"))
        s_gates = [sem(f"s_gates{c}") for c in range(CPART)]
        s_gate, s_up, s_silu, s_y, s_yc, s_yh, s_yl, s_down = (
            sem("s_gate"), sem("s_up"), sem("s_silu"), sem("s_y"), sem("s_yc"), sem("s_yh"), sem("s_yl"),
            sem("s_down"))
        s_final, s_out = sem("s_final"), sem("s_out")

        block = ctx.enter_context(nc.Block())
        KEY_PARTS = [(0, KEYS), (KEYS, B * KEYS)]

        def bcast(ap, n):
            return ap.unsqueeze(2).to_broadcast([P, J, n])

        @block.sync
        def _(sp):
            sp.dma_start(fpack[:], first_pack).then_inc(s_fpack, 16)
            sp.dma_start(wq[:], wq_rows).then_inc(s_wq, 16)
            sp.dma_start(x[:, 0:J, :], x_rows[:, 0:J * D]).then_inc(s_rows[0], 16)
            sp.dma_start(xT[:, 0, :], x_cols[:, 0:T]).then_inc(s_cols[0], 16)
            sp.dma_start(lpack[:], later_pack).then_inc(s_lpack, 16)
            sp.dma_start(bv[:], bv_row.to_broadcast([KEYS, D])).then_inc(s_bv, 16)

            def load_w1(e):
                sp.dma_start(w1_raw[:, e, :], w1_cols[:, e * 4 * P:(e + 1) * 4 * P]).then_inc(s_w1[e], 16)

            def load_w2(part):
                half = E // 2
                sp.dma_start(w2_raw[:, part * half:(part + 1) * half, :],
                             w2_cols[:, part * half * 2 * D:(part + 1) * half * 2 * D]).then_inc(s_w2[part], 16)

            def store(b):
                sp.wait_ge(s_final, b + 1)
                sp.dma_start(out[:, b * T:(b + 1) * T], out_sb[:, b % 2, :]).then_inc(s_out, 16)

            def load_rows(b):
                sp.dma_start(x[:, b * J:(b + 1) * J, :],
                             x_rows[:, b * J * D:(b + 1) * J * D]).then_inc(s_rows[b], 16)

            def load_cols(b):
                sp.dma_start(xT[:, b, :], x_cols[:, b * T:(b + 1) * T]).then_inc(s_cols[b], 16)

            load_rows(1)
            load_w1(0)
            load_rows(2)
            load_rows(3)
            load_cols(1)
            load_w1(1)
            load_cols(2)
            load_cols(3)
            load_w2(0)
            for e in range(2, E):
                load_w1(e)
            load_w2(1)

            for b in range(B):
                sp.wait_ge(s_combT, b + 1)
                sp.dma_start(comb_dram[b, :, :], combT[:]).then_inc(s_comb_out, 16)
                sp.wait_ge(s_comb_out, 16 * (b + 1))
                if b >= 1:
                    sp.wait_ge(s_yc, S * b)
                for c in range(CPART):
                    if b == 0:
                        sp.wait_ge(s_w1lo, (c + 1) * EP)
                    src = comb_dram[b, c * EP * J:(c + 1) * EP * J, :].rearrange("r p -> (r p)")
                    sp.dma_start(gates[:, c * EP:(c + 1) * EP, :].rearrange("p e t -> p (e t)"),
                                 src.unsqueeze(0).to_broadcast([P, EP * T])).then_inc(s_gates[c], 16)
                if b >= 1:
                    store(b - 1)
            store(B - 1)
            sp.wait_ge(s_out, 16 * B)

        @block.gpsimd
        def _(pool):
            nc.gpsimd.memset(ident[:], 0.0).then_inc(s_ident0, 1)
            nc.gpsimd.memset(half_neg[:], -0.5).then_inc(s_half, 1)
            pool.wait_ge(s_ident0, 1)
            nc.gpsimd.affine_select(out=ident[:], in_=ident[:], compare_op=ALU.not_equal, fill=1.0, base=0,
                                    pattern=[[-1, P]], channel_multiplier=1).then_inc(s_ident, 1)

            pool.wait_ge(s_half, 1)

            def inverse_std(variance, v_eps, r_std, s_mid, n_mid, s_done, n_done):
                nc.gpsimd.tensor_scalar(v_eps, variance, EPS, None, ALU.add).then_inc(s_mid, n_done)
                pool.wait_ge(s_mid, n_mid)
                nc.gpsimd.tensor_tensor(r_std, v_eps, half_neg[:, 0:n_done], ALU.pow).then_inc(s_done, n_done)

            def first_norm(b):
                r = slice(b * J, (b + 1) * J)
                pool.wait_ge(s_mv, J * (b + 1))
                inverse_std(mv[:, r, 1], veps[:, r], rstd[:, r], s_veps, J * (b + 1), s_rstd, J)

            def second_norm(b):
                if b >= 1:
                    pool.wait_ge(s_xn2, J * b)
                for part in parts(b):
                    r, done = slice(part.start, part.stop), J * b + part.stop
                    pool.wait_ge(s_mv2, done)
                    inverse_std(mv2[:, r, 1], veps2[:, r], rstd2[:, r], s_veps2, done, s_rstd2, len(part))

            def split_w1(e):
                pool.wait_ge(s_w1[e], 16)
                pool.wait_ge(s_w1hi, e + 1)
                nc.gpsimd.tensor_tensor(w1_lo[:, e, :], w1_raw[:, e, :], w1_hi[:, e, :].bitcast(fp32),
                                        ALU.subtract).then_inc(s_w1lo, 1)

            def split_w2(e):
                pool.wait_ge(s_w2[e // (E // 2)], 16)
                pool.wait_ge(s_w2hi, e + 1)
                nc.gpsimd.tensor_tensor(w2_lo[:, e, :], w2_raw[:, e, :], w2_hi[:, e, :].bitcast(fp32),
                                        ALU.subtract).then_inc(s_w2lo, 1)

            first_norm(0)
            first_norm(1)
            split_w1(0)
            first_norm(2)
            first_norm(3)
            second_norm(0)
            for e in range(1, E):
                split_w1(e)
                if e == NORM_AT:
                    second_norm(1)

            for b in range(B):
                if 1 <= b < B - 1:
                    second_norm(b + 1)
                for s in range(S):
                    g = S * b + s
                    if s % (S // CPART) == 0:
                        pool.wait_ge(s_gates[s // (S // CPART)], 16 * (b + 1))
                    if b == 0 and s < E:
                        split_w2(s)
                    pool.wait_ge(s_y, g + 1)
                    nc.gpsimd.tensor_tensor(y[:, g % NY, :], y[:, g % NY, :], gates[:, s // 2, :],
                                            ALU.mult).then_inc(s_yc, 1)

        @block.scalar
        def _(act):
            act.wait_ge(s_ones, 1)
            nc.scalar.activation(act_warm[:], ones[:, 0:1], ACT.Exp)

            def move_k(i):
                a, z = KEY_PARTS[i]
                act.wait_ge(s_kT_ps, i + 1)
                nc.scalar.activation(kT[:, a:z], kT_ps[:, a:z], ACT.Identity, bias=bk).then_inc(s_kT, 1)

            def move_keys(i):
                a, z = KEY_PARTS[i]
                act.wait_ge(s_m_ps, i + 1)
                nc.scalar.activation(mT[:, a:z], m_ps[:, a:z], ACT.Copy).then_inc(s_mT, 1)
                act.wait_ge(s_cb_ps, i + 1)
                nc.scalar.activation(cbias[:, a:z], cb_ps[:, a:z], ACT.Copy).then_inc(s_cbias, 1)

            def softmax_exp(b):
                if b >= 1:
                    r = slice(b * J, (b + 1) * J)
                    act.wait_ge(s_shift, b)
                    nc.scalar.activation(attn[:, r, :], attn[:, r, :], ACT.Exp).then_inc(s_exp, J)
                    return
                for j in range(J):
                    act.wait_ge(s_nmax, j + 1)
                    nc.scalar.activation(attn[:, j, :], attn[:, j, :], ACT.Exp, bias=nmax[:, j:j + 1],
                                         accum_out=esum[:, j:j + 1]).then_inc(s_exp, 1)

            def scale_scores(b):
                act.wait_ge(s_score_ps, b + 1)
                act.wait_ge(s_rstd, J * (b + 1))
                for j in range(J):
                    n = b * J + j
                    last = nc.scalar.activation(attn[:, n, :], scores_ps[b][:, j * KEYS:(j + 1) * KEYS], ACT.Copy,
                                                scale=rstd[:, n:n + 1])
                last.then_inc(s_scaled, 1)

            def w1_round(e):
                act.wait_ge(s_w1[e], 16)
                nc.scalar.activation(w1_hi[:, e, :], w1_raw[:, e, :], ACT.Copy).then_inc(s_w1hi, 1)

            def w2_round(e):
                act.wait_ge(s_w2[e // (E // 2)], 16)
                nc.scalar.activation(w2_hi[:, e, :], w2_raw[:, e, :], ACT.Copy).then_inc(s_w2hi, 1)

            def move_eT(b):
                if b >= 1:
                    act.wait_ge(s_av, J * b)
                for part in parts(b):
                    t = slice(part.start * P, part.stop * P)
                    act.wait_ge(s_eT_ps, J * b + part.stop)
                    nc.scalar.activation(eT[:, t], attn_bank(b, part.start)[0:KEYS, t],
                                         ACT.Copy).then_inc(s_eT, len(part))

            def move_x2T(b):
                act.wait_ge(s_x2T_ps, b + 1)
                nc.scalar.activation(x2T[:, b, :], bank_o[:], ACT.Copy).then_inc(s_x2T, 1)

            def round_x(b, part):
                t = slice(part.start * P, part.stop * P)
                act.wait_ge(s_xnT_ps, J * b + part.stop)
                nc.scalar.activation(xh[:, b % 2, t], attn_bank(b, part.start)[:, t],
                                     ACT.Copy).then_inc(s_xh, len(part))

            def router_tanh(b):
                act.wait_ge(s_dist, b + 1)
                if b >= 1:
                    act.wait_ge(s_prob, b)
                nc.scalar.activation(tanh_h[:], dist[:], ACT.Tanh, scale=0.5).then_inc(s_tanh, 1)

            def move_combT(b):
                act.wait_ge(s_combT_ps, b + 1)
                if b >= 1:
                    act.wait_ge(s_comb_out, 16 * b)
                nc.scalar.activation(combT[:], bank_r[0:E * J, 0:P], ACT.Copy).then_inc(s_combT, 1)

            def silu_step(g):
                act.wait_ge(s_gate, g + 1)
                if g >= SIL:
                    act.wait_ge(s_y, g - SIL + 1)
                nc.scalar.activation(silu[:, g % SIL, :], gate_ps[g % 2][:], ACT.Silu).then_inc(s_silu, 1)

            def round_y(g):
                act.wait_ge(s_yc, g + 1)
                if g >= NS:
                    act.wait_ge(s_down, g - NS + 1)
                nc.scalar.activation(y_hi[:, g % NS, :], y[:, g % NY, :], ACT.Copy).then_inc(s_yh, 1)

            move_k(0)
            move_keys(0)
            w1_round(0)
            move_k(1)
            softmax_exp(0)
            move_eT(0)
            move_keys(1)
            w1_round(1)
            scale_scores(1)
            scale_scores(2)
            first, second = parts(0)
            round_x(0, first)
            w1_round(2)
            round_x(0, second)
            scale_scores(3)
            softmax_exp(1)

            for b in range(B):
                for s in range(S):
                    g = S * b + s
                    silu_step(g)
                    if g == 0:
                        router_tanh(0)
                    if g == 1:
                        move_x2T(0)
                    if g == EXP_AT:
                        for later in range(2, B):
                            softmax_exp(later)
                    if b == 0 and s < E - 3:
                        w1_round(s + 3)
                    if b == 0 and E - 3 <= s < 2 * E - 3:
                        w2_round(s - E + 3)
                    if g >= SPLIT_LAG:
                        round_y(g - SPLIT_LAG)
                    if s == (COMB_AT if b else FIRST_COMB_AT):
                        move_combT(b)
                    if b + 1 < B:
                        if s == 1:
                            move_eT(b + 1)
                        if s == 6:
                            move_x2T(b + 1)
                        if s == 9:
                            round_x(b + 1, range(J))
                        if s == 12:
                            router_tanh(b + 1)
            for g in range(S * B - SPLIT_LAG, S * B):
                round_y(g)

        @block.vector
        def _(dve):
            nc.vector.memset(ones[:], 1.0).then_inc(s_ones, 1)
            for e in range(E):
                last = nc.vector.memset(order[:, :, e], float(E - e))
            last.then_inc(s_order, 1)

            def first_stats(b):
                dve.wait_ge(s_rows[b], 16)
                for j in range(b * J, (b + 1) * J):
                    nc.vector.bn_stats(st[:, j, :], x[:, j, :]).then_inc(s_st, 1)
                for j in range(b * J, (b + 1) * J):
                    dve.wait_ge(s_st, j + 1)
                    nc.vector.bn_aggr(mv[:, j, :], st[:, j, :]).then_inc(s_mv, 1)

            def centre_wq():
                dve.wait_ge(s_wq, 16)
                nc.vector.tensor_scalar(wq_scaled[:], wq[:], 1.0 / D, None, ALU.mult, ALU.add,
                                        accum_out=wq_mean[:]).then_inc(s_wqmean, 1)
                dve.wait_ge(s_wqmean, 1)
                nc.vector.tensor_scalar(wq_c[:], wq[:], wq_mean[:], None, ALU.subtract).then_inc(s_wqc, 1)
                dve.wait_ge(s_fpack, 16)
                dve.wait_ge(s_ones, 1)
                nc.vector.tensor_scalar(bq_rep[:], ones[:], bq, None, ALU.mult).then_inc(s_bqrep, 1)

            def split_router():
                dve.wait_ge(s_lpack, 16)
                nc.vector.tensor_copy(wr[:, 0, :], wrT).then_inc(s_wrhi, 1)
                dve.wait_ge(s_wrhi, 1)
                nc.vector.tensor_tensor(wr[:, 1, :], wrT, wr[:, 0, :].bitcast(fp32), ALU.subtract).then_inc(s_wrlo, 1)

            def move_v():
                dve.wait_ge(s_v_ps, 1)
                dve.wait_ge(s_bv, 16)
                nc.vector.tensor_tensor(v[:], v_ps[0:KEYS, :].rearrange("k (b d) -> k b d", d=D),
                                        bv[:].unsqueeze(1).to_broadcast([KEYS, B, D]), ALU.add).then_inc(s_v, 1)

            def first_scores():
                dve.wait_ge(s_score_ps, 1)
                dve.wait_ge(s_rstd, J)
                dve.wait_ge(s_cbias, 1)
                for j in range(J):
                    nc.vector.scalar_tensor_tensor(
                        out=attn[:, j, :], in0=scores_ps[0][:, j * KEYS:(j + 1) * KEYS], scalar=rstd[:, j:j + 1],
                        in1=cbias[:, 0:KEYS], op0=ALU.mult, op1=ALU.add).then_inc(s_score, 1)

            def score_max(b):
                for part in parts(b):
                    r = slice(b * J + part.start, b * J + part.stop)
                    dve.wait_ge(s_score, r.stop)
                    nc.vector.tensor_reduce(nmax[:, r], attn[:, r, :], AX.X, ALU.max,
                                            negate=True).then_inc(s_nmax, len(part))

            def add_bias(b):
                r = slice(b * J, (b + 1) * J)
                dve.wait_ge(s_scaled, b)
                dve.wait_ge(s_cbias, 2)
                bias = cbias[:, b * KEYS:(b + 1) * KEYS].unsqueeze(1).to_broadcast([P, J, KEYS])
                nc.vector.tensor_tensor(attn[:, r, :], attn[:, r, :], bias, ALU.add).then_inc(s_score, J)

            def shift_scores(b):
                r = slice(b * J, (b + 1) * J)
                dve.wait_ge(s_nmax, r.stop)
                nc.vector.tensor_tensor(attn[:, r, :], attn[:, r, :], bcast(nmax[:, r], KEYS),
                                        ALU.add).then_inc(s_shift, 1)

            def sum_exp(b):
                r = slice(b * J, (b + 1) * J)
                dve.wait_ge(s_exp, r.stop)
                nc.vector.tensor_reduce(esum[:, r], attn[:, r, :], AX.X, ALU.add).then_inc(s_esum, 1)

            def invert_sum(b):
                if b == 0:
                    dve.wait_ge(s_exp, J)
                else:
                    dve.wait_ge(s_esum, b)
                nc.vector.reciprocal(rsum[:, b * J:(b + 1) * J], esum[:, b * J:(b + 1) * J]).then_inc(s_rsum, 1)

            def attend(b, part):
                dve.wait_ge(s_av, J * b + part.stop)
                dve.wait_ge(s_rsum, b + 1)
                if b >= 1:
                    dve.wait_ge(s_x2T_ps, b)
                for j in part:
                    n = b * J + j
                    nc.vector.scalar_tensor_tensor(
                        out=x2[:, j, :], in0=value_bank(b, j)[:, j * D:(j + 1) * D], scalar=rsum[:, n:n + 1],
                        in1=x[:, n, :], op0=ALU.mult, op1=ALU.add).then_inc(s_x2, 1)

            def second_stats(b, part):
                if b >= 1:
                    dve.wait_ge(s_veps2, J * b)
                for j in part:
                    dve.wait_ge(s_x2, J * b + j + 1)
                    nc.vector.bn_stats(st2[:, j, :], x2[:, j, :]).then_inc(s_st2, 1)
                for j in part:
                    dve.wait_ge(s_st2, J * b + j + 1)
                    nc.vector.bn_aggr(mv2[:, j, :], st2[:, j, :]).then_inc(s_mv2, 1)

            def normalise(b, part):
                dve.wait_ge(s_rstd2, J * b + part.stop)
                if b >= 1:
                    dve.wait_ge(s_xnT_ps, J * b)
                for j in part:
                    nc.vector.tensor_scalar(xn2[:, j, :], x2[:, j, :], mv2[:, j, 0:1], rstd2[:, j:j + 1],
                                            ALU.subtract, ALU.mult).then_inc(s_xn2, 1)

            def split_x(b, part):
                t = slice(part.start * P, part.stop * P)
                dve.wait_ge(s_xh, J * b + part.stop)
                nc.vector.tensor_tensor(xl[:, b % 2, t], attn_bank(b, part.start)[:, t],
                                        xh[:, b % 2, t].bitcast(fp32), ALU.subtract).then_inc(s_xl, len(part))

            logit_parts = bank_r[:, 0:J * 2 * E].rearrange("p (j h e) -> p j e h", h=2, e=E)

            def r_logits(b):
                dve.wait_ge(s_logit_ps, b + 1)
                nc.vector.tensor_reduce(logits[:], logit_parts, AX.X, ALU.add).then_inc(s_logits, 1)

            def r_top(b):
                dve.wait_ge(s_logits, b + 1)
                nc.vector.tensor_reduce(top[:], logits[:], AX.X, ALU.max).then_inc(s_top, 1)

            def r_dist(b):
                dve.wait_ge(s_top, b + 1)
                nc.vector.tensor_tensor(dist[:], logits[:], bcast(top[:], E), ALU.subtract).then_inc(s_dist, 1)

            def r_mark1(b):
                dve.wait_ge(s_dist, b + 1)
                nc.vector.scalar_tensor_tensor(out=mark1[:], in0=dist[:], scalar=0.0, in1=order[:],
                                               op0=ALU.is_equal, op1=ALU.mult).then_inc(s_mark1, 1)

            def r_first1(b):
                dve.wait_ge(s_mark1, b + 1)
                nc.vector.tensor_reduce(first1[:], mark1[:], AX.X, ALU.max).then_inc(s_first1, 1)

            def r_pick1(b):
                dve.wait_ge(s_first1, b + 1)
                nc.vector.tensor_tensor(pick1[:], mark1[:], bcast(first1[:], E), ALU.is_equal).then_inc(s_pick1, 1)

            def r_rest0(b):
                dve.wait_ge(s_pick1, b + 1)
                nc.vector.scalar_tensor_tensor(out=rest0[:], in0=pick1[:], scalar=-FAR, in1=dist[:],
                                               op0=ALU.mult, op1=ALU.add).then_inc(s_rest0, 1)

            def r_top2(b):
                dve.wait_ge(s_rest0, b + 1)
                nc.vector.tensor_reduce(top2[:], rest0[:], AX.X, ALU.max).then_inc(s_top2, 1)

            def r_rest(b):
                dve.wait_ge(s_top2, b + 1)
                nc.vector.tensor_tensor(rest[:], rest0[:], bcast(top2[:], E), ALU.is_equal).then_inc(s_rest, 1)

            def r_mark2(b):
                dve.wait_ge(s_rest, b + 1)
                nc.vector.tensor_tensor(mark2[:], rest[:], order[:], ALU.mult).then_inc(s_mark2, 1)

            def r_first2(b):
                dve.wait_ge(s_mark2, b + 1)
                nc.vector.tensor_reduce(first2[:], mark2[:], AX.X, ALU.max).then_inc(s_first2, 1)

            def r_pick2(b):
                dve.wait_ge(s_first2, b + 1)
                nc.vector.tensor_tensor(pick2[:], mark2[:], bcast(first2[:], E), ALU.is_equal).then_inc(s_pick2, 1)

            def r_picks(b):
                dve.wait_ge(s_pick2, b + 1)
                nc.vector.tensor_tensor(picks[:], pick1[:], pick2[:], ALU.add).then_inc(s_picks, 1)

            def r_den(b):
                dve.wait_ge(s_tanh, b + 1)
                nc.vector.tensor_scalar(den[:], tanh_h[:], -1.0, 1.0, ALU.mult, ALU.add).then_inc(s_den, 1)

            def r_rden(b):
                dve.wait_ge(s_den, b + 1)
                nc.vector.reciprocal(rden[:], den[:]).then_inc(s_rden, 1)

            def r_prob(b):
                dve.wait_ge(s_rden, b + 1)
                nc.vector.scalar_tensor_tensor(out=prob[:], in0=tanh_h[:], scalar=1.0, in1=rden[:],
                                               op0=ALU.add, op1=ALU.mult).then_inc(s_prob, 1)

            def r_psum(b):
                dve.wait_ge(s_prob, b + 1)
                nc.vector.tensor_reduce(psum_e[:], prob[:], AX.X, ALU.add).then_inc(s_psum, 1)

            def r_rpsum(b):
                dve.wait_ge(s_psum, b + 1)
                nc.vector.reciprocal(rpsum[:], psum_e[:]).then_inc(s_rpsum, 1)

            def r_probn(b):
                dve.wait_ge(s_rpsum, b + 1)
                nc.vector.tensor_tensor(probn[:], prob[:], bcast(rpsum[:], E), ALU.mult).then_inc(s_probn, 1)

            def r_comb(b):
                dve.wait_ge(s_picks, b + 1)
                dve.wait_ge(s_probn, b + 1)
                if b >= 1:
                    dve.wait_ge(s_combT_ps, b)
                nc.vector.tensor_tensor(comb[:].rearrange("p e j -> p j e"), picks[:], probn[:],
                                        ALU.mult).then_inc(s_comb, 1)

            def multiply(g):
                dve.wait_ge(s_up, g + 1)
                dve.wait_ge(s_silu, g + 1)
                if g >= NY:
                    dve.wait_ge(s_yl, g - NY + 1)
                nc.vector.tensor_tensor(y[:, g % NY, :], up_ps[g % 2][:], silu[:, g % SIL, :],
                                        ALU.mult).then_inc(s_y, 1)

            def split_y(g):
                dve.wait_ge(s_yh, g + 1)
                if g >= NS:
                    dve.wait_ge(s_down, g - NS + 1)
                nc.vector.tensor_tensor(y_lo[:, g % NS, :], y[:, g % NY, :], y_hi[:, g % NS, :].bitcast(fp32),
                                        ALU.subtract).then_inc(s_yl, 1)

            def finish(b):
                dve.wait_ge(s_down, S * (b + 1))
                dve.wait_ge(s_x2T, b + 1)
                if b >= 2:
                    dve.wait_ge(s_out, 16 * (b - 1))
                nc.vector.tensor_tensor(out_sb[:, b % 2, :], out_ps[:], x2T[:, b, :], ALU.add).then_inc(s_final, 1)

            def router_slot(b, slot):
                if slot == 0:
                    r_logits(b)
                    r_top(b)
                    r_dist(b)
                if slot == 1:
                    r_mark1(b)
                    r_first1(b)
                if slot == 2:
                    r_pick1(b)
                    r_den(b)
                    r_rest0(b)
                    r_rden(b)
                if slot == 3:
                    r_top2(b)
                    r_prob(b)
                    r_rest(b)
                    r_psum(b)
                if slot == 4:
                    r_mark2(b)
                    r_rpsum(b)
                    r_first2(b)
                    r_probn(b)
                if slot == 5:
                    r_pick2(b)
                    r_picks(b)
                if slot == 6:
                    r_comb(b)

            centre_wq()
            first_stats(0)
            first_stats(1)
            first_scores()
            score_max(0)
            first_stats(2)
            move_v()
            invert_sum(0)
            first_stats(3)
            for part in parts(0):
                attend(0, part)
                second_stats(0, part)
            first, second = parts(0)
            normalise(0, first)
            split_router()
            add_bias(1)
            normalise(0, second)
            split_x(0, first)
            score_max(1)
            split_x(0, second)
            shift_scores(1)
            dve.wait_ge(s_order, 1)
            r_logits(0)
            r_top(0)
            r_dist(0)
            r_mark1(0)
            r_first1(0)
            r_pick1(0)

            for b in range(B):
                for s in range(S):
                    g = S * b + s
                    multiply(g)
                    if g == 0:
                        r_rest0(0)
                        r_den(0)
                        r_top2(0)
                        r_rden(0)
                        r_rest(0)
                    if g == 1:
                        r_prob(0)
                        r_mark2(0)
                        r_psum(0)
                        r_first2(0)
                        r_rpsum(0)
                    if g == 2:
                        r_pick2(0)
                        r_probn(0)
                        r_picks(0)
                        r_comb(0)
                    if b + 1 < B:
                        if s == 4:
                            second_stats(b + 1, range(J))
                        if s == 7:
                            normalise(b + 1, range(J))
                        if s == 10:
                            split_x(b + 1, range(J))
                        if s >= 12:
                            router_slot(b + 1, 2 * (s - 12))
                    if b >= 1 and s == OUT_LAG - 1:
                        finish(b - 1)
                    if g >= SPLIT_LAG:
                        split_y(g - SPLIT_LAG)
                    if g == EXP_AT - 5:
                        for later in range(2, B):
                            add_bias(later)
                    if g == EXP_AT - 3:
                        for later in range(2, B):
                            score_max(later)
                    if g == EXP_AT - 2:
                        for later in range(2, B):
                            shift_scores(later)
                    if b + 1 < B:
                        if s == 2:
                            sum_exp(b + 1)
                            invert_sum(b + 1)
                        if s == 3:
                            attend(b + 1, range(J))
                        if 12 <= s < 15:
                            router_slot(b + 1, 2 * (s - 12) + 1)
            for g in range(S * B - SPLIT_LAG, S * B):
                split_y(g)
            finish(B - 1)

        @block.tensor
        def _(pe):
            def project_keys(i):
                a, z = KEY_PARTS[i]
                nc.tensor.matmul(kT_ps[:, a:z], wkT, context(a, z), start=True, stop=True).then_inc(s_kT_ps, 1)

            def fold_query(i):
                a, z = KEY_PARTS[i]
                pe.wait_ge(s_kT, i + 1)
                if i >= 1:
                    pe.wait_ge(s_mT, i)
                    pe.wait_ge(s_cbias, i)
                nc.tensor.matmul(m_ps[:, a:z], wq_c[:], kT[:, a:z], start=True, stop=True).then_inc(s_m_ps, 1)
                pe.wait_ge(s_bqrep, 1)
                nc.tensor.matmul(cb_ps[:, a:z], bq_rep[:], kT[:, a:z], start=True, stop=True).then_inc(s_cb_ps, 1)

            def project_values():
                for b in range(B):
                    last = nc.tensor.matmul(v_ps[0:KEYS, b * D:(b + 1) * D], context(b * KEYS, (b + 1) * KEYS),
                                            wvT, start=True, stop=True)
                last.then_inc(s_v_ps, 1)

            def score(b):
                pe.wait_ge(s_cols[b], 16)
                pe.wait_ge(s_mT, 1 if b == 0 else 2)
                for j in range(J):
                    last = nc.tensor.matmul(scores_ps[b][:, j * KEYS:(j + 1) * KEYS], xT[:, b, j * P:(j + 1) * P],
                                            mT[:, b * KEYS:(b + 1) * KEYS], start=True, stop=True)
                last.then_inc(s_score_ps, 1)

            def transpose_attn(b):
                if b >= 1:
                    pe.wait_ge(s_xl, J * b)
                for j in range(J):
                    pe.wait_ge(s_exp, J * (b if b == 0 else b + 1) + (j + 1 if b == 0 else 0))
                    nc.tensor.transpose(attn_bank(b, j)[0:KEYS, j * P:(j + 1) * P], attn[:, b * J + j, :],
                                        ident[:]).then_inc(s_eT_ps, 1)

            def weigh_values(b):
                pe.wait_ge(s_v, 1)
                if b >= 1:
                    pe.wait_ge(s_x2T, b)
                for part in parts(b):
                    pe.wait_ge(s_eT, J * b + part.stop)
                    for j in part:
                        nc.tensor.matmul(value_bank(b, j)[:, j * D:(j + 1) * D], eT[:, j * P:(j + 1) * P], v[:, b, :],
                                         start=True, stop=True).then_inc(s_av, 1)

            def transpose_x2(b):
                pe.wait_ge(s_x2, J * (b + 1))
                for j in range(J):
                    last = nc.tensor.transpose(bank_o[:, j * P:(j + 1) * P], x2[:, j, :], ident[:])
                last.then_inc(s_x2T_ps, 1)

            def transpose_xn(b):
                for part in parts(b):
                    pe.wait_ge(s_xn2, J * b + part.stop)
                    for j in part:
                        nc.tensor.transpose(attn_bank(b, j)[:, j * P:(j + 1) * P], xn2[:, j, :],
                                            ident[:]).then_inc(s_xnT_ps, 1)

            def route(b):
                pe.wait_ge(s_xl, J * (b + 1))
                pe.wait_ge(s_wrlo, 1)
                if b >= 1:
                    pe.wait_ge(s_combT, b)
                for j in range(J):
                    o = bank_r[:, j * 2 * E:(j + 1) * 2 * E]
                    t = slice(j * P, (j + 1) * P)
                    nc.tensor.matmul(o, xh[:, b % 2, t], wr[:].rearrange("d h e -> d (h e)"), start=True, stop=False)
                    last = nc.tensor.matmul(o[:, 0:E], xl[:, b % 2, t], wr[:, 0, :], start=False, stop=True)
                last.then_inc(s_logit_ps, 1)

            def transpose_comb(b):
                pe.wait_ge(s_comb, b + 1)
                nc.tensor.transpose(bank_r[0:E * J, 0:P], comb[:].rearrange("p e j -> p (e j)"),
                                    ident[:]).then_inc(s_combT_ps, 1)

            def expand(b, s):
                g = S * b + s
                e, h = s // 2, s % 2
                if b == 0:
                    pe.wait_ge(s_w1lo, e + 1)
                    if s == 1:
                        pe.wait_ge(s_scaled, B - 1)
                if s == 0:
                    pe.wait_ge(s_xl, J * (b + 1))
                for o, at, free, done in ((gate_ps[g % 2], 2 * h, s_silu, s_gate), (up_ps[g % 2], 2 * h + 1, s_y, s_up)):
                    if g >= BANKS:
                        pe.wait_ge(free, g - BANKS + 1)
                    c = slice(at * P, (at + 1) * P)
                    nc.tensor.matmul(o[:], w1_hi[:, e, c], xh[:, b % 2, :], start=True, stop=False)
                    nc.tensor.matmul(o[:], w1_hi[:, e, c], xl[:, b % 2, :], start=False, stop=False)
                    nc.tensor.matmul(o[:], w1_lo[:, e, c], xh[:, b % 2, :], start=False, stop=True).then_inc(done, 1)

            def expand_first():
                gate_at, up_at = slice(0, P), slice(P, 2 * P)
                pe.wait_ge(s_w1lo, 1)
                for part in parts(0):
                    t = slice(part.start * P, part.stop * P)
                    pe.wait_ge(s_xh, part.stop)
                    for o, c in ((gate_ps[0], gate_at), (up_ps[0], up_at)):
                        nc.tensor.matmul(o[:, t], w1_hi[:, 0, c], xh[:, 0, t], start=True, stop=False)
                        nc.tensor.matmul(o[:, t], w1_lo[:, 0, c], xh[:, 0, t], start=False, stop=False)
                    pe.wait_ge(s_xl, part.stop)
                    gate_done = nc.tensor.matmul(gate_ps[0][:, t], w1_hi[:, 0, gate_at], xl[:, 0, t], start=False,
                                                 stop=True)
                    up_done = nc.tensor.matmul(up_ps[0][:, t], w1_hi[:, 0, up_at], xl[:, 0, t], start=False,
                                               stop=True)
                gate_done.then_inc(s_gate, 1)
                up_done.then_inc(s_up, 1)

            def contract(g):
                b, s = g // S, g % S
                e, h = s // 2, s % 2
                pe.wait_ge(s_yl, g + 1)
                if b == 0:
                    pe.wait_ge(s_w2lo, e + 1)
                if s == 0:
                    if b >= 1:
                        pe.wait_ge(s_final, b)
                c = slice(h * D, (h + 1) * D)
                nc.tensor.matmul(out_ps[:], w2_hi[:, e, c], y_hi[:, g % NS, :], start=s == 0, stop=False)
                nc.tensor.matmul(out_ps[:], w2_hi[:, e, c], y_lo[:, g % NS, :], start=False, stop=False)
                nc.tensor.matmul(out_ps[:], w2_lo[:, e, c], y_hi[:, g % NS, :], start=False,
                                 stop=s == S - 1).then_inc(s_down, 1)

            pe.wait_ge(s_fpack, 16)
            project_keys(0)
            pe.wait_ge(s_wqc, 1)
            fold_query(0)
            score(0)
            pe.wait_ge(s_lpack, 16)
            project_keys(1)
            project_values()
            pe.wait_ge(s_ident, 1)
            transpose_attn(0)
            fold_query(1)
            weigh_values(0)
            score(1)
            pe.wait_ge(s_cbias, 2)
            score(2)
            pe.wait_ge(s_x2, J)
            score(3)
            transpose_x2(0)
            transpose_xn(0)

            for b in range(B):
                for s in range(S):
                    g = S * b + s
                    if g == 0:
                        expand_first()
                        route(0)
                    else:
                        expand(b, s)
                    if g >= OUT_LAG:
                        contract(g - OUT_LAG)
                    if s == (COMB_AT if b else FIRST_COMB_AT):
                        transpose_comb(b)
                    if b + 1 < B:
                        if s == 1:
                            transpose_attn(b + 1)
                        if s == 3:
                            weigh_values(b + 1)
                        if s == 6:
                            transpose_x2(b + 1)
                        if s == 9:
                            transpose_xn(b + 1)
                        if s == 11:
                            route(b + 1)
            for g in range(S * B - OUT_LAG, S * B):
                contract(g)


def kernel(**inputs):
    import numpy as np
    import concourse.bacc as bacc
    from concourse.bass_utils import run_bass_kernel_spmd

    x = np.asarray(inputs["x"])
    context = np.asarray(inputs["ctx_1024"])
    B, T, D = x.shape
    w1 = np.asarray(inputs["L0_ffn_w1"])
    w2 = np.asarray(inputs["L0_ffn_w2"])
    E = w1.shape[0]
    P = 128
    tokens = x.reshape(B * T, D)
    arrays = {
        "x_rows": tokens.reshape(B * T // P, P, D).transpose(1, 0, 2).reshape(P, -1),
        "x_cols": tokens.T,
        "first_pack": np.concatenate([context[0].T, np.asarray(inputs["L0_xattn_Wk"]).T,
                                      np.asarray(inputs["L0_xattn_bk"])[:, None],
                                      np.asarray(inputs["L0_xattn_bq"])[:, None]], axis=1),
        "wq_rows": np.asarray(inputs["L0_xattn_Wq"]),
        "later_pack": np.concatenate([context[1:].reshape(-1, D).T, np.asarray(inputs["L0_xattn_Wv"]).T,
                                      np.asarray(inputs["L0_ffn_router_w"]).T], axis=1),
        "bv_row": np.asarray(inputs["L0_xattn_bv"])[None, :],
        "w1_cols": w1.reshape(E, 2, 2, P, D).transpose(4, 0, 2, 1, 3).reshape(D, -1),
        "w2_cols": w2.reshape(E, D, 2, P).transpose(3, 0, 2, 1).reshape(P, -1),
    }
    arrays = {name: np.ascontiguousarray(a) for name, a in arrays.items()}

    nc = bacc.Bacc("TRN2", target_bir_lowering=False, num_devices=1)
    args = {name: nc.dram_tensor(name, a.shape, mybir.dt.from_np(a.dtype), kind="ExternalInput").ap()
            for name, a in arrays.items()}
    out = nc.dram_tensor("out", (D, B * T), mybir.dt.float32, kind="ExternalOutput").ap()
    xattn_moe_kernel(nc, out=out, **args)
    r = run_bass_kernel_spmd(nc, [arrays], core_ids=[0])
    return np.ascontiguousarray(r.results[0]["out"].T).reshape(B, T, D)
```

```python
import concourse.bass as bass
from concourse import mybir
from contextlib import ExitStack


def xattn_moe_kernel(
    nc: bass.Bass,
    x_rows: bass.AP,
    x_cols: bass.AP,
    first_pack: bass.AP,
    wq_rows: bass.AP,
    later_pack: bass.AP,
    bv_row: bass.AP,
    w1_cols: bass.AP,
    w2_cols: bass.AP,
    out: bass.AP,
):
    fp32 = mybir.dt.float32
    fp32r = mybir.dt.float32r
    ALU = mybir.AluOpType
    ACT = mybir.ActivationFunctionType
    AX = mybir.AxisListType

    P = 128
    D = 128
    E = w2_cols.shape[1] // (2 * D)
    T = 512
    B = x_cols.shape[1] // T
    J = T // P
    KEYS = first_pack.shape[1] - D - 2
    S = 2 * E
    EPS = 1e-5
    FAR = 1e30

    BANKS = 2
    SIL = 4
    NY = S
    NS = 4
    SPLIT_LAG = 10
    OUT_LAG = 12
    CPART = 4
    EP = E // CPART
    EXP_AT = 14
    FIRST_COMB_AT = 4
    COMB_AT = 1
    CLOSE_AT = S - 3
    NORM_AFTER = E - 1

    ctx = ExitStack()
    with ctx:
        def sb(name, shape, dt=fp32):
            return ctx.enter_context(nc.sbuf_tensor(name, shape, dt))

        def sem(name):
            return ctx.enter_context(nc.semaphore(name))

        x = sb("x", [P, B * J, D])
        xT = sb("xT", [D, B, T])
        fpack = sb("fpack", [D, KEYS + D + 2])
        wq = sb("wq", [D, D])
        lpack = sb("lpack", [D, (B - 1) * KEYS + D + E])
        bv = sb("bv", [KEYS, D])
        wkT = fpack[:, KEYS:KEYS + D]
        bk = fpack[:, KEYS + D:KEYS + D + 1]
        bq = fpack[:, KEYS + D + 1:KEYS + D + 2]
        wvT = lpack[:, (B - 1) * KEYS:(B - 1) * KEYS + D]
        wrT = lpack[:, (B - 1) * KEYS + D:(B - 1) * KEYS + D + E]

        def context(a, z):
            return fpack[:, a:z] if z <= KEYS else lpack[:, a - KEYS:z - KEYS]

        ident = sb("ident", [P, P])
        ones = sb("ones", [P, P])
        half_neg = sb("half_neg", [P, J])
        order = sb("order", [P, J, E])
        dve_pause = sb("dve_pause", [P, 1])
        act_pause = sb("act_pause", [P, 1])
        act_warm = sb("act_warm", [P, 1])

        wq_mean = sb("wq_mean", [D, 1])
        wq_scaled = sb("wq_scaled", [D, D])
        wq_c = sb("wq_c", [D, D])
        bq_rep = sb("bq_rep", [D, P])
        kT = sb("kT", [D, B * KEYS])
        mT = sb("mT", [D, B * KEYS])
        cbias = sb("cbias", [P, B * KEYS])
        v = sb("v", [KEYS, B, D])

        st = sb("st", [P, B * J, 6])
        mv = sb("mv", [P, B * J, 2])
        veps = sb("veps", [P, B * J])
        rstd = sb("rstd", [P, B * J])
        attn = sb("attn", [P, B * J, KEYS])
        attn_now = sb("attn_now", [P, J, KEYS])
        nmax = sb("nmax", [P, B * J])
        esum = sb("esum", [P, B * J])
        rsum = sb("rsum", [P, B * J])
        eT = sb("eT", [KEYS, T])
        x2 = sb("x2", [P, J, D])
        st2 = sb("st2", [P, J, 6])
        mv2 = sb("mv2", [P, J, 2])
        veps2 = sb("veps2", [P, J])
        rstd2 = sb("rstd2", [P, J])
        xn2 = sb("xn2", [P, J, D])
        x2T = sb("x2T", [D, B, T])
        xh = sb("xh", [D, 2, T], fp32r)
        xl = sb("xl", [D, 2, T], fp32r)

        xr = sb("xr", [D, 2, T], fp32r)
        wr = sb("wr", [D, 2, E], fp32r)
        w1_hi = sb("w1_hi", [D, E, 4 * P], fp32r)
        w1_lo = sb("w1_lo", [D, E, 4 * P], fp32r)
        w2_hi = sb("w2_hi", [P, E, 2 * D], fp32r)
        w2_lo = sb("w2_lo", [P, E, 2 * D], fp32r)
        w2_raw = sb("w2_raw", [P, E, 2 * D])
        gates = sb("gates", [P, E, T])
        w1_raw = gates[:]

        top = sb("top", [P, J])
        top2 = sb("top2", [P, J])
        first1 = sb("first1", [P, J])
        first2 = sb("first2", [P, J])
        logits = sb("logits", [P, J, E])
        dist = sb("dist", [P, J, E])
        rest = sb("rest", [P, J, E])
        rest0 = sb("rest0", [P, J, E])
        mark1 = sb("mark1", [P, J, E])
        mark2 = sb("mark2", [P, J, E])
        pick1 = sb("pick1", [P, J, E])
        pick2 = sb("pick2", [P, J, E])
        picks = sb("picks", [P, J, E])
        tanh_h = sb("tanh_h", [P, J, E])
        den = sb("den", [P, J, E])
        rden = sb("rden", [P, J, E])
        prob = sb("prob", [P, J, E])
        psum_e = sb("psum_e", [P, J])
        rpsum = sb("rpsum", [P, J])
        probn = sb("probn", [P, J, E])
        comb = sb("comb", [P, E, J])
        combT = sb("combT", [E * J, P])

        silu = sb("silu", [P, SIL, T])
        y = sb("y", [P, NY, T])
        y_hi = sb("y_hi", [P, NS, T], fp32r)
        y_lo = sb("y_lo", [P, NS, T], fp32r)
        out_sb = sb("out_sb", [D, T])

        comb_dram = nc.dram_tensor("comb_scratch", (B, E * J, P), fp32).ap()

        bank = [ctx.enter_context(nc.psum_tensor(f"bank{i}", [P, T], fp32)) for i in range(8)]
        gate_ps = bank[0:2]
        up_ps = bank[2:4]
        out_ps = bank[4]
        bank_e, bank_o, bank_r = bank[5], bank[6], bank[7]
        kT_ps, v_ps, m_ps, cb_ps = bank[0], bank[1], bank[2], bank[3]
        scores_ps = [bank_e, out_ps, bank[3], bank[1]]

        def each_batch(engine, body):
            body(0)
            with engine.Fori(1, B - 1) as b:
                body(b)
            body(B - 1)

        def in_loop(b):
            return not isinstance(b, int)

        def is_first(b):
            return not in_loop(b) and b == 0

        def is_last(b):
            return not in_loop(b) and b == B - 1

        def slot(b):
            return b % 2

        def before(b, s, lag):
            return (b, s - lag) if s >= lag else (b - 1, s - lag + S)

        def splits_at(b, s):
            if is_first(b) and s < SPLIT_LAG:
                return []
            if is_last(b) and s == CLOSE_AT:
                return [before(b, s, SPLIT_LAG), before(b, s, SPLIT_LAG - 1)]
            return [before(b, s, SPLIT_LAG - 1 if is_last(b) and s > CLOSE_AT else SPLIT_LAG)]

        def turn_at(b):
            return 9 if is_first(b) else 8

        def parts(b):
            return [range(0, J // 2), range(J // 2, J)] if is_first(b) else [range(J)]

        def attn_bank(b, j):
            return bank_r if is_first(b) and j >= J // 2 else bank_e

        def value_bank(b, j):
            return bank[1] if is_first(b) and j >= J // 2 else bank_o

        s_fpack, s_wq, s_lpack, s_bv = sem("s_fpack"), sem("s_wq"), sem("s_lpack"), sem("s_bv")
        s_rows = [sem(f"s_rows{b}") for b in range(B)]
        s_cols = [sem(f"s_cols{b}") for b in range(B)]
        s_w1 = [sem(f"s_w1_{e}") for e in range(E)]
        s_w2 = [sem(f"s_w2_{e}") for e in range(2)]
        s_ident0, s_ident, s_ones, s_half, s_order = (
            sem("s_ident0"), sem("s_ident"), sem("s_ones"), sem("s_half"), sem("s_order"))
        s_wqmean, s_wqc, s_bqrep = sem("s_wqmean"), sem("s_wqc"), sem("s_bqrep")
        s_kT_ps, s_kT = sem("s_kT_ps"), sem("s_kT")
        s_v_ps, s_v = sem("s_v_ps"), sem("s_v")
        s_m_ps, s_mT = sem("s_m_ps"), sem("s_mT")
        s_cb_ps, s_cbias = sem("s_cb_ps"), sem("s_cbias")
        s_wrhi, s_wrlo = sem("s_wrhi"), sem("s_wrlo")
        s_w1hi, s_w1lo, s_w2hi, s_w2lo = sem("s_w1hi"), sem("s_w1lo"), sem("s_w2hi"), sem("s_w2lo")
        s_st, s_mv, s_veps, s_rstd = sem("s_st"), sem("s_mv"), sem("s_veps"), sem("s_rstd")
        s_score_ps, s_score, s_nmax, s_exp, s_rsum = (
            sem("s_score_ps"), sem("s_score"), sem("s_nmax"), sem("s_exp"), sem("s_rsum"))
        s_staged, s_xr = sem("s_staged"), sem("s_xr")
        s_scaled, s_shift, s_esum = sem("s_scaled"), sem("s_shift"), sem("s_esum")
        s_eT_ps, s_eT, s_av = sem("s_eT_ps"), sem("s_eT"), sem("s_av")
        s_x2, s_st2, s_mv2, s_veps2, s_rstd2, s_xn2 = (
            sem("s_x2"), sem("s_st2"), sem("s_mv2"), sem("s_veps2"), sem("s_rstd2"), sem("s_xn2"))
        s_x2T_ps, s_x2T, s_xnT_ps, s_xh, s_xl = (
            sem("s_x2T_ps"), sem("s_x2T"), sem("s_xnT_ps"), sem("s_xh"), sem("s_xl"))
        s_logit_ps, s_logits, s_top, s_dist, s_tanh = sem("s_logit_ps"), sem("s_logits"), sem("s_top"), sem("s_dist"), sem("s_tanh")
        s_mark1, s_first1, s_pick1, s_rest0, s_top2, s_rest, s_mark2, s_first2, s_pick2, s_picks = (
            sem("s_mark1"), sem("s_first1"), sem("s_pick1"), sem("s_rest0"), sem("s_top2"), sem("s_rest"),
            sem("s_mark2"), sem("s_first2"), sem("s_pick2"), sem("s_picks"))
        s_den, s_rden, s_prob, s_psum, s_rpsum, s_probn = (
            sem("s_den"), sem("s_rden"), sem("s_prob"), sem("s_psum"), sem("s_rpsum"), sem("s_probn"))
        s_comb, s_combT_ps, s_combT, s_comb_out = (
            sem("s_comb"), sem("s_combT_ps"), sem("s_combT"), sem("s_comb_out"))
        s_gates = [sem(f"s_gates{c}") for c in range(CPART)]
        s_gate, s_up, s_silu, s_y, s_yc, s_yh, s_yl, s_down = (
            sem("s_gate"), sem("s_up"), sem("s_silu"), sem("s_y"), sem("s_yc"), sem("s_yh"), sem("s_yl"),
            sem("s_down"))
        s_final, s_out = sem("s_final"), sem("s_out")

        block = ctx.enter_context(nc.Block())
        KEY_PARTS = [(0, KEYS), (KEYS, B * KEYS)]

        def bcast(ap, n):
            return ap.unsqueeze(2).to_broadcast([P, J, n])

        @block.sync
        def _(sp):
            sp.dma_start(fpack[:], first_pack).then_inc(s_fpack, 16)
            sp.dma_start(wq[:], wq_rows).then_inc(s_wq, 16)
            sp.dma_start(x[:, 0:J, :], x_rows[:, 0:J * D]).then_inc(s_rows[0], 16)
            sp.dma_start(xT[:, 0, :], x_cols[:, 0:T]).then_inc(s_cols[0], 16)
            sp.dma_start(lpack[:], later_pack).then_inc(s_lpack, 16)
            sp.dma_start(bv[:], bv_row.to_broadcast([KEYS, D])).then_inc(s_bv, 16)

            def load_w1(e):
                sp.dma_start(w1_raw[:, e, :], w1_cols[:, e * 4 * P:(e + 1) * 4 * P]).then_inc(s_w1[e], 16)

            def load_w2(part):
                half = E // 2
                sp.dma_start(w2_raw[:, part * half:(part + 1) * half, :],
                             w2_cols[:, part * half * 2 * D:(part + 1) * half * 2 * D]).then_inc(s_w2[part], 16)

            def store(b):
                sp.wait_ge(s_final, b + 1)
                sp.dma_start(out[:, b * T:(b + 1) * T], out_sb[:]).then_inc(s_out, 16)

            def load_rows(b):
                sp.dma_start(x[:, b * J:(b + 1) * J, :],
                             x_rows[:, b * J * D:(b + 1) * J * D]).then_inc(s_rows[b], 16)

            def load_cols(b):
                sp.dma_start(xT[:, b, :], x_cols[:, b * T:(b + 1) * T]).then_inc(s_cols[b], 16)

            load_rows(1)
            load_w1(0)
            load_rows(2)
            load_rows(3)
            load_cols(1)
            load_w1(1)
            load_cols(2)
            load_cols(3)
            load_w2(0)
            for e in range(2, E):
                load_w1(e)
            load_w2(1)

            for b in range(B):
                sp.wait_ge(s_combT, b + 1)
                sp.dma_start(comb_dram[b, :, :], combT[:]).then_inc(s_comb_out, 16)
                sp.wait_ge(s_comb_out, 16 * (b + 1))
                if not is_first(b):
                    sp.wait_ge(s_yc, S * b)
                for c in range(CPART):
                    if b == 0:
                        sp.wait_ge(s_w1lo, (c + 1) * EP)
                    src = comb_dram[b, c * EP * J:(c + 1) * EP * J, :].rearrange("r p -> (r p)")
                    sp.dma_start(gates[:, c * EP:(c + 1) * EP, :].rearrange("p e t -> p (e t)"),
                                 src.unsqueeze(0).to_broadcast([P, EP * T])).then_inc(s_gates[c], 16)
                if not is_first(b):
                    store(b - 1)
            for half in range(2):
                t = slice(half * T // 2, (half + 1) * T // 2)
                sp.wait_ge(s_final, B + half)
                sp.dma_start(out[:, (B - 1) * T + t.start:(B - 1) * T + t.stop], out_sb[:, t]).then_inc(s_out, 16)
            sp.wait_ge(s_out, 16 * (B + 1))

        @block.gpsimd
        def _(pool):
            nc.gpsimd.memset(ident[:], 0.0).then_inc(s_ident0, 1)
            nc.gpsimd.memset(half_neg[:], -0.5).then_inc(s_half, 1)
            pool.wait_ge(s_ident0, 1)
            nc.gpsimd.affine_select(out=ident[:], in_=ident[:], compare_op=ALU.not_equal, fill=1.0, base=0,
                                    pattern=[[-1, P]], channel_multiplier=1).then_inc(s_ident, 1)

            pool.wait_ge(s_half, 1)

            def inverse_std(variance, v_eps, r_std, s_mid, n_mid, s_done, n_done):
                nc.gpsimd.tensor_scalar(v_eps, variance, EPS, None, ALU.add).then_inc(s_mid, n_done)
                pool.wait_ge(s_mid, n_mid)
                nc.gpsimd.tensor_tensor(r_std, v_eps, half_neg[:, 0:n_done], ALU.pow).then_inc(s_done, n_done)

            def first_norm(b):
                r = slice(b * J, (b + 1) * J)
                pool.wait_ge(s_mv, J * (b + 1))
                inverse_std(mv[:, r, 1], veps[:, r], rstd[:, r], s_veps, J * (b + 1), s_rstd, J)

            def second_norm(b):
                if not is_first(b):
                    pool.wait_ge(s_xn2, J * b)
                for part in parts(b):
                    r, done = slice(part.start, part.stop), J * b + part.stop
                    pool.wait_ge(s_mv2, done)
                    inverse_std(mv2[:, r, 1], veps2[:, r], rstd2[:, r], s_veps2, done, s_rstd2, len(part))

            def split_w1(e):
                pool.wait_ge(s_w1[e], 16)
                pool.wait_ge(s_w1hi, e + 1)
                nc.gpsimd.tensor_tensor(w1_lo[:, e, :], w1_raw[:, e, :], w1_hi[:, e, :].bitcast(fp32),
                                        ALU.subtract).then_inc(s_w1lo, 1)

            def split_w2(e):
                pool.wait_ge(s_w2[e // (E // 2)], 16)
                pool.wait_ge(s_w2hi, e + 1)
                nc.gpsimd.tensor_tensor(w2_lo[:, e, :], w2_raw[:, e, :], w2_hi[:, e, :].bitcast(fp32),
                                        ALU.subtract).then_inc(s_w2lo, 1)

            first_norm(0)
            first_norm(1)
            split_w1(0)
            first_norm(2)
            first_norm(3)
            second_norm(0)
            for e in range(1, E):
                split_w1(e)
                if e == NORM_AFTER:
                    second_norm(1)

            def batch(b):
                if not is_first(b) and not is_last(b):
                    second_norm(b + 1)
                for s in range(S):
                    if s % (S // CPART) == 0:
                        pool.wait_ge(s_gates[s // (S // CPART)], 16 * (b + 1))
                    if is_first(b) and s < E:
                        split_w2(s)
                    pool.wait_ge(s_y, S * b + s + 1)
                    nc.gpsimd.tensor_tensor(y[:, s % NY, :], y[:, s % NY, :], gates[:, s // 2, :],
                                            ALU.mult).then_inc(s_yc, 1)

            each_batch(pool, batch)

        @block.scalar
        def _(act):
            act.wait_ge(s_ones, 1)
            nc.scalar.activation(act_warm[:], ones[:, 0:1], ACT.Exp)

            def move_k(i):
                a, z = KEY_PARTS[i]
                act.wait_ge(s_kT_ps, i + 1)
                nc.scalar.activation(kT[:, a:z], kT_ps[:, a:z], ACT.Identity, bias=bk).then_inc(s_kT, 1)

            def move_keys(i):
                a, z = KEY_PARTS[i]
                act.wait_ge(s_m_ps, i + 1)
                nc.scalar.activation(mT[:, a:z], m_ps[:, a:z], ACT.Copy).then_inc(s_mT, 1)
                act.wait_ge(s_cb_ps, i + 1)
                nc.scalar.activation(cbias[:, a:z], cb_ps[:, a:z], ACT.Copy).then_inc(s_cbias, 1)

            def softmax_exp(b):
                if not is_first(b):
                    r = slice(b * J, (b + 1) * J)
                    act.wait_ge(s_shift, b)
                    nc.scalar.activation(attn[:, r, :], attn[:, r, :], ACT.Exp).then_inc(s_exp, J)
                    return
                for j in range(J):
                    act.wait_ge(s_nmax, j + 1)
                    nc.scalar.activation(attn[:, j, :], attn[:, j, :], ACT.Exp, bias=nmax[:, j:j + 1],
                                         accum_out=esum[:, j:j + 1]).then_inc(s_exp, 1)

            def scale_scores(b):
                act.wait_ge(s_score_ps, b + 1)
                act.wait_ge(s_rstd, J * (b + 1))
                for j in range(J):
                    n = b * J + j
                    last = nc.scalar.activation(attn[:, n, :], scores_ps[b][:, j * KEYS:(j + 1) * KEYS], ACT.Copy,
                                                scale=rstd[:, n:n + 1])
                last.then_inc(s_scaled, 1)

            def w1_round(e):
                act.wait_ge(s_w1[e], 16)
                nc.scalar.activation(w1_hi[:, e, :], w1_raw[:, e, :], ACT.Copy).then_inc(s_w1hi, 1)

            def w2_round(e):
                act.wait_ge(s_w2[e // (E // 2)], 16)
                nc.scalar.activation(w2_hi[:, e, :], w2_raw[:, e, :], ACT.Copy).then_inc(s_w2hi, 1)

            def stage_attn(b):
                act.wait_ge(s_exp, J * (b + 1))
                act.wait_ge(s_eT_ps, J * b)
                nc.scalar.activation(attn_now[:], attn[:, bass.ds(b * J, J), :], ACT.Copy).then_inc(s_staged, 1)

            def move_eT(b):
                if not is_first(b):
                    act.wait_ge(s_av, J * b)
                for part in parts(b):
                    t = slice(part.start * P, part.stop * P)
                    act.wait_ge(s_eT_ps, J * b + part.stop)
                    nc.scalar.activation(eT[:, t], attn_bank(b, part.start)[0:KEYS, t],
                                         ACT.Copy).then_inc(s_eT, len(part))

            def move_x2T(b):
                act.wait_ge(s_x2T_ps, b + 1)
                nc.scalar.activation(x2T[:, b, :], bank_o[:], ACT.Copy).then_inc(s_x2T, 1)

            def round_x(b, part):
                t = slice(part.start * P, part.stop * P)
                act.wait_ge(s_xnT_ps, J * b + part.stop)
                nc.scalar.activation(xh[:, slot(b), t], attn_bank(b, part.start)[:, t],
                                     ACT.Copy).then_inc(s_xh, len(part))

            def stage_x(b, i):
                act.wait_ge((s_xh, s_xl)[i], J * (b + 1))
                act.wait_ge(s_logit_ps, b)
                nc.scalar.activation(act_pause[:], ones[:, 0:1], ACT.Copy)
                nc.scalar.activation(xr[:, i, :], (xh, xl)[i][:, slot(b), :].bitcast(fp32), ACT.Copy).then_inc(s_xr, 1)

            def router_tanh(b):
                act.wait_ge(s_dist, b + 1)
                if not is_first(b):
                    act.wait_ge(s_prob, b)
                nc.scalar.activation(tanh_h[:], dist[:], ACT.Tanh, scale=0.5).then_inc(s_tanh, 1)

            def move_combT(b):
                act.wait_ge(s_combT_ps, b + 1)
                if not is_first(b):
                    act.wait_ge(s_comb_out, 16 * b)
                nc.scalar.activation(combT[:], bank_r[0:E * J, 0:P], ACT.Copy).then_inc(s_combT, 1)

            def silu_step(b, s):
                act.wait_ge(s_gate, S * b + s + 1)
                if not is_first(b) or s >= SIL:
                    act.wait_ge(s_y, S * b + s - SIL + 1)
                nc.scalar.activation(silu[:, s % SIL, :], gate_ps[s % 2][:], ACT.Silu).then_inc(s_silu, 1)

            def round_y(b, s):
                act.wait_ge(s_yc, S * b + s + 1)
                if not is_first(b) or s >= NS:
                    act.wait_ge(s_down, S * b + s - NS + 1)
                nc.scalar.activation(y_hi[:, s % NS, :], y[:, s % NY, :], ACT.Copy).then_inc(s_yh, 1)

            move_k(0)
            move_keys(0)
            w1_round(0)
            move_k(1)
            softmax_exp(0)
            move_eT(0)
            move_keys(1)
            w1_round(1)
            scale_scores(1)
            scale_scores(2)
            first, second = parts(0)
            round_x(0, first)
            w1_round(2)
            round_x(0, second)
            scale_scores(3)
            softmax_exp(1)

            def batch(b):
                for s in range(S):
                    silu_step(b, s)
                    if is_first(b) and s == 0:
                        router_tanh(0)
                    if is_first(b) and s == 1:
                        move_x2T(0)
                    if is_first(b) and s == EXP_AT:
                        for later in range(2, B):
                            softmax_exp(later)
                    if is_first(b) and s < E - 3:
                        w1_round(s + 3)
                    if is_first(b) and E - 3 <= s < 2 * E - 3:
                        w2_round(s - E + 3)
                    for earlier in splits_at(b, s):
                        round_y(*earlier)
                    if s == (FIRST_COMB_AT if is_first(b) else COMB_AT):
                        move_combT(b)
                    if not is_last(b):
                        if in_loop(b) and s == 0:
                            stage_attn(b + 1)
                        if s == 1:
                            move_eT(b + 1)
                        if s == 6:
                            move_x2T(b + 1)
                        if s == turn_at(b):
                            round_x(b + 1, range(J))
                            if in_loop(b):
                                stage_x(b + 1, 0)
                        if in_loop(b) and s == turn_at(b) + 1:
                            stage_x(b + 1, 1)
                        if s == 12:
                            router_tanh(b + 1)

            each_batch(act, batch)
            for s in range(S - SPLIT_LAG + 1, S):
                round_y(B - 1, s)

        @block.vector
        def _(dve):
            nc.vector.memset(ones[:], 1.0).then_inc(s_ones, 1)
            for e in range(E):
                last = nc.vector.memset(order[:, :, e], float(E - e))
            last.then_inc(s_order, 1)

            def first_stats(b):
                dve.wait_ge(s_rows[b], 16)
                for j in range(b * J, (b + 1) * J):
                    nc.vector.bn_stats(st[:, j, :], x[:, j, :]).then_inc(s_st, 1)
                for j in range(b * J, (b + 1) * J):
                    dve.wait_ge(s_st, j + 1)
                    nc.vector.bn_aggr(mv[:, j, :], st[:, j, :]).then_inc(s_mv, 1)

            def centre_wq():
                dve.wait_ge(s_wq, 16)
                nc.vector.tensor_scalar(wq_scaled[:], wq[:], 1.0 / D, None, ALU.mult, ALU.add,
                                        accum_out=wq_mean[:]).then_inc(s_wqmean, 1)
                dve.wait_ge(s_wqmean, 1)
                nc.vector.tensor_scalar(wq_c[:], wq[:], wq_mean[:], None, ALU.subtract).then_inc(s_wqc, 1)
                dve.wait_ge(s_fpack, 16)
                dve.wait_ge(s_ones, 1)
                nc.vector.tensor_scalar(bq_rep[:], ones[:], bq, None, ALU.mult).then_inc(s_bqrep, 1)

            def split_router():
                dve.wait_ge(s_lpack, 16)
                nc.vector.tensor_copy(wr[:, 0, :], wrT).then_inc(s_wrhi, 1)
                dve.wait_ge(s_wrhi, 1)
                nc.vector.tensor_tensor(wr[:, 1, :], wrT, wr[:, 0, :].bitcast(fp32), ALU.subtract).then_inc(s_wrlo, 1)

            def move_v():
                dve.wait_ge(s_v_ps, 1)
                dve.wait_ge(s_bv, 16)
                nc.vector.tensor_tensor(v[:], v_ps[0:KEYS, :].rearrange("k (b d) -> k b d", d=D),
                                        bv[:].unsqueeze(1).to_broadcast([KEYS, B, D]), ALU.add).then_inc(s_v, 1)

            def first_scores():
                dve.wait_ge(s_score_ps, 1)
                dve.wait_ge(s_rstd, J)
                dve.wait_ge(s_cbias, 1)
                for j in range(J):
                    nc.vector.scalar_tensor_tensor(
                        out=attn[:, j, :], in0=scores_ps[0][:, j * KEYS:(j + 1) * KEYS], scalar=rstd[:, j:j + 1],
                        in1=cbias[:, 0:KEYS], op0=ALU.mult, op1=ALU.add).then_inc(s_score, 1)

            def score_max(b):
                for part in parts(b):
                    r = slice(b * J + part.start, b * J + part.stop)
                    dve.wait_ge(s_score, r.stop)
                    nc.vector.tensor_reduce(nmax[:, r], attn[:, r, :], AX.X, ALU.max,
                                            negate=True).then_inc(s_nmax, len(part))

            def add_bias(b):
                r = slice(b * J, (b + 1) * J)
                dve.wait_ge(s_scaled, b)
                dve.wait_ge(s_cbias, 2)
                bias = cbias[:, b * KEYS:(b + 1) * KEYS].unsqueeze(1).to_broadcast([P, J, KEYS])
                nc.vector.tensor_tensor(attn[:, r, :], attn[:, r, :], bias, ALU.add).then_inc(s_score, J)

            def shift_scores(b):
                r = slice(b * J, (b + 1) * J)
                dve.wait_ge(s_nmax, r.stop)
                nc.vector.tensor_tensor(attn[:, r, :], attn[:, r, :], bcast(nmax[:, r], KEYS),
                                        ALU.add).then_inc(s_shift, 1)

            def sum_exp(b):
                r = bass.ds(b * J, J)
                dve.wait_ge(s_exp, J * (b + 1))
                nc.vector.tensor_reduce(esum[:, r], attn[:, r, :], AX.X, ALU.add).then_inc(s_esum, 1)

            def invert_sum(b):
                if is_first(b):
                    dve.wait_ge(s_exp, J)
                else:
                    dve.wait_ge(s_esum, b)
                r = bass.ds(b * J, J)
                nc.vector.reciprocal(rsum[:, r], esum[:, r]).then_inc(s_rsum, 1)

            def attend(b, part):
                dve.wait_ge(s_av, J * b + part.stop)
                dve.wait_ge(s_rsum, b + 1)
                if not is_first(b):
                    dve.wait_ge(s_x2T_ps, b)
                for j in part:
                    n = b * J + j
                    nc.vector.scalar_tensor_tensor(
                        out=x2[:, j, :], in0=value_bank(b, j)[:, j * D:(j + 1) * D], scalar=rsum[:, bass.ds(n, 1)],
                        in1=x[:, n, :], op0=ALU.mult, op1=ALU.add).then_inc(s_x2, 1)

            def second_stats(b, part):
                if not is_first(b):
                    dve.wait_ge(s_veps2, J * b)
                for j in part:
                    dve.wait_ge(s_x2, J * b + j + 1)
                    nc.vector.bn_stats(st2[:, j, :], x2[:, j, :]).then_inc(s_st2, 1)
                dve.wait_ge(s_st2, J * b + part.stop)
                nc.vector.memset(dve_pause[:], 0.0)
                for j in part:
                    nc.vector.bn_aggr(mv2[:, j, :], st2[:, j, :]).then_inc(s_mv2, 1)

            def normalise(b, part):
                dve.wait_ge(s_rstd2, J * b + part.stop)
                if not is_first(b):
                    dve.wait_ge(s_xnT_ps, J * b)
                for j in part:
                    nc.vector.tensor_scalar(xn2[:, j, :], x2[:, j, :], mv2[:, j, 0:1], rstd2[:, j:j + 1],
                                            ALU.subtract, ALU.mult).then_inc(s_xn2, 1)

            def split_x(b, part):
                t = slice(part.start * P, part.stop * P)
                dve.wait_ge(s_xh, J * b + part.stop)
                nc.vector.tensor_tensor(xl[:, slot(b), t], attn_bank(b, part.start)[:, t],
                                        xh[:, slot(b), t].bitcast(fp32), ALU.subtract).then_inc(s_xl, len(part))

            logit_parts = bank_r[:, 0:J * 2 * E].rearrange("p (j h e) -> p j e h", h=2, e=E)

            def r_logits(b):
                dve.wait_ge(s_logit_ps, b + 1)
                nc.vector.tensor_reduce(logits[:], logit_parts, AX.X, ALU.add).then_inc(s_logits, 1)

            def r_top(b):
                dve.wait_ge(s_logits, b + 1)
                nc.vector.tensor_reduce(top[:], logits[:], AX.X, ALU.max).then_inc(s_top, 1)

            def r_dist(b):
                dve.wait_ge(s_top, b + 1)
                nc.vector.tensor_tensor(dist[:], logits[:], bcast(top[:], E), ALU.subtract).then_inc(s_dist, 1)

            def r_mark1(b):
                dve.wait_ge(s_dist, b + 1)
                nc.vector.scalar_tensor_tensor(out=mark1[:], in0=dist[:], scalar=0.0, in1=order[:],
                                               op0=ALU.is_equal, op1=ALU.mult).then_inc(s_mark1, 1)

            def r_first1(b):
                dve.wait_ge(s_mark1, b + 1)
                nc.vector.tensor_reduce(first1[:], mark1[:], AX.X, ALU.max).then_inc(s_first1, 1)

            def r_pick1(b):
                dve.wait_ge(s_first1, b + 1)
                nc.vector.tensor_tensor(pick1[:], mark1[:], bcast(first1[:], E), ALU.is_equal).then_inc(s_pick1, 1)

            def r_rest0(b):
                dve.wait_ge(s_pick1, b + 1)
                nc.vector.scalar_tensor_tensor(out=rest0[:], in0=pick1[:], scalar=-FAR, in1=dist[:],
                                               op0=ALU.mult, op1=ALU.add).then_inc(s_rest0, 1)

            def r_top2(b):
                dve.wait_ge(s_rest0, b + 1)
                nc.vector.tensor_reduce(top2[:], rest0[:], AX.X, ALU.max).then_inc(s_top2, 1)

            def r_rest(b):
                dve.wait_ge(s_top2, b + 1)
                nc.vector.tensor_tensor(rest[:], rest0[:], bcast(top2[:], E), ALU.is_equal).then_inc(s_rest, 1)

            def r_mark2(b):
                dve.wait_ge(s_rest, b + 1)
                nc.vector.tensor_tensor(mark2[:], rest[:], order[:], ALU.mult).then_inc(s_mark2, 1)

            def r_first2(b):
                dve.wait_ge(s_mark2, b + 1)
                nc.vector.tensor_reduce(first2[:], mark2[:], AX.X, ALU.max).then_inc(s_first2, 1)

            def r_pick2(b):
                dve.wait_ge(s_first2, b + 1)
                nc.vector.tensor_tensor(pick2[:], mark2[:], bcast(first2[:], E), ALU.is_equal).then_inc(s_pick2, 1)

            def r_picks(b):
                dve.wait_ge(s_pick2, b + 1)
                nc.vector.tensor_tensor(picks[:], pick1[:], pick2[:], ALU.add).then_inc(s_picks, 1)

            def r_den(b):
                dve.wait_ge(s_tanh, b + 1)
                nc.vector.tensor_scalar(den[:], tanh_h[:], -1.0, 1.0, ALU.mult, ALU.add).then_inc(s_den, 1)

            def r_rden(b):
                dve.wait_ge(s_den, b + 1)
                nc.vector.reciprocal(rden[:], den[:]).then_inc(s_rden, 1)

            def r_prob(b):
                dve.wait_ge(s_rden, b + 1)
                nc.vector.scalar_tensor_tensor(out=prob[:], in0=tanh_h[:], scalar=1.0, in1=rden[:],
                                               op0=ALU.add, op1=ALU.mult).then_inc(s_prob, 1)

            def r_psum(b):
                dve.wait_ge(s_prob, b + 1)
                nc.vector.tensor_reduce(psum_e[:], prob[:], AX.X, ALU.add).then_inc(s_psum, 1)

            def r_rpsum(b):
                dve.wait_ge(s_psum, b + 1)
                nc.vector.reciprocal(rpsum[:], psum_e[:]).then_inc(s_rpsum, 1)

            def r_probn(b):
                dve.wait_ge(s_rpsum, b + 1)
                nc.vector.tensor_tensor(probn[:], prob[:], bcast(rpsum[:], E), ALU.mult).then_inc(s_probn, 1)

            def r_comb(b):
                dve.wait_ge(s_picks, b + 1)
                dve.wait_ge(s_probn, b + 1)
                if not is_first(b):
                    dve.wait_ge(s_combT_ps, b)
                nc.vector.tensor_tensor(comb[:].rearrange("p e j -> p j e"), picks[:], probn[:],
                                        ALU.mult).then_inc(s_comb, 1)

            def multiply(b, s):
                dve.wait_ge(s_up, S * b + s + 1)
                dve.wait_ge(s_silu, S * b + s + 1)
                if not is_first(b):
                    dve.wait_ge(s_yl, S * b + s - NY + 1)
                nc.vector.tensor_tensor(y[:, s % NY, :], up_ps[s % 2][:], silu[:, s % SIL, :],
                                        ALU.mult).then_inc(s_y, 1)

            def split_y(b, s):
                dve.wait_ge(s_yh, S * b + s + 1)
                if not is_first(b) or s >= NS:
                    dve.wait_ge(s_down, S * b + s - NS + 1)
                nc.vector.tensor_tensor(y_lo[:, s % NS, :], y[:, s % NY, :], y_hi[:, s % NS, :].bitcast(fp32),
                                        ALU.subtract).then_inc(s_yl, 1)

            def finish(b):
                dve.wait_ge(s_down, S * (b + 1))
                dve.wait_ge(s_x2T, b + 1)
                if not is_first(b):
                    dve.wait_ge(s_out, 16 * b)
                pieces = 2 if is_last(b) else 1
                for i in range(pieces):
                    t = slice(i * T // pieces, (i + 1) * T // pieces)
                    nc.vector.tensor_tensor(out_sb[:, t], out_ps[:, t], x2T[:, b, t], ALU.add).then_inc(s_final, 1)

            def router_slot(b, part):
                if part == 0:
                    r_logits(b)
                    r_top(b)
                    r_dist(b)
                if part == 1:
                    r_mark1(b)
                    r_first1(b)
                if part == 2:
                    r_pick1(b)
                    r_den(b)
                    r_rest0(b)
                    r_rden(b)
                if part == 3:
                    r_top2(b)
                    r_prob(b)
                    r_rest(b)
                    r_psum(b)
                if part == 4:
                    r_mark2(b)
                    r_rpsum(b)
                    r_first2(b)
                    r_probn(b)
                if part == 5:
                    r_pick2(b)
                    r_picks(b)
                if part == 6:
                    r_comb(b)

            centre_wq()
            first_stats(0)
            first_stats(1)
            first_scores()
            score_max(0)
            first_stats(2)
            move_v()
            invert_sum(0)
            first_stats(3)
            for part in parts(0):
                attend(0, part)
                second_stats(0, part)
            first, second = parts(0)
            normalise(0, first)
            split_router()
            add_bias(1)
            normalise(0, second)
            split_x(0, first)
            score_max(1)
            split_x(0, second)
            shift_scores(1)
            dve.wait_ge(s_order, 1)
            r_logits(0)
            r_top(0)
            r_dist(0)
            r_mark1(0)
            r_first1(0)
            r_pick1(0)

            def batch(b):
                for s in range(S):
                    multiply(b, s)
                    if is_first(b) and s == 0:
                        r_rest0(0)
                        r_den(0)
                        r_top2(0)
                        r_rden(0)
                        r_rest(0)
                    if is_first(b) and s == 1:
                        r_prob(0)
                        r_mark2(0)
                        r_psum(0)
                        r_first2(0)
                        r_rpsum(0)
                    if is_first(b) and s == 2:
                        r_pick2(0)
                        r_probn(0)
                        r_picks(0)
                        r_comb(0)
                    if not is_last(b):
                        if s == 4:
                            second_stats(b + 1, range(J))
                        if s == 7:
                            normalise(b + 1, range(J))
                        if s == turn_at(b) + 1:
                            split_x(b + 1, range(J))
                        if s >= 12:
                            router_slot(b + 1, 2 * (s - 12))
                    if not is_first(b) and s == OUT_LAG - 1:
                        finish(b - 1)
                    for earlier in splits_at(b, s):
                        split_y(*earlier)
                    if is_first(b) and s == EXP_AT - 5:
                        for later in range(2, B):
                            add_bias(later)
                    if is_first(b) and s == EXP_AT - 3:
                        for later in range(2, B):
                            score_max(later)
                    if is_first(b) and s == EXP_AT - 2:
                        for later in range(2, B):
                            shift_scores(later)
                    if not is_last(b):
                        if s == 2:
                            sum_exp(b + 1)
                            invert_sum(b + 1)
                        if s == 3:
                            attend(b + 1, range(J))
                        if 12 <= s < 15:
                            router_slot(b + 1, 2 * (s - 12) + 1)

            each_batch(dve, batch)
            for s in range(S - SPLIT_LAG + 1, S):
                split_y(B - 1, s)
            finish(B - 1)

        @block.tensor
        def _(pe):
            def project_keys(i):
                a, z = KEY_PARTS[i]
                nc.tensor.matmul(kT_ps[:, a:z], wkT, context(a, z), start=True, stop=True).then_inc(s_kT_ps, 1)

            def fold_query(i):
                a, z = KEY_PARTS[i]
                pe.wait_ge(s_kT, i + 1)
                if i >= 1:
                    pe.wait_ge(s_mT, i)
                    pe.wait_ge(s_cbias, i)
                nc.tensor.matmul(m_ps[:, a:z], wq_c[:], kT[:, a:z], start=True, stop=True).then_inc(s_m_ps, 1)
                pe.wait_ge(s_bqrep, 1)
                nc.tensor.matmul(cb_ps[:, a:z], bq_rep[:], kT[:, a:z], start=True, stop=True).then_inc(s_cb_ps, 1)

            def project_values():
                for b in range(B):
                    last = nc.tensor.matmul(v_ps[0:KEYS, b * D:(b + 1) * D], context(b * KEYS, (b + 1) * KEYS),
                                            wvT, start=True, stop=True)
                last.then_inc(s_v_ps, 1)

            def score(b):
                pe.wait_ge(s_cols[b], 16)
                pe.wait_ge(s_mT, 1 if is_first(b) else 2)
                for j in range(J):
                    last = nc.tensor.matmul(scores_ps[b][:, j * KEYS:(j + 1) * KEYS], xT[:, b, j * P:(j + 1) * P],
                                            mT[:, b * KEYS:(b + 1) * KEYS], start=True, stop=True)
                last.then_inc(s_score_ps, 1)

            def transpose_attn(b):
                if not is_first(b):
                    pe.wait_ge(s_xl, J * b)
                if in_loop(b):
                    pe.wait_ge(s_staged, b - 1)
                for j in range(J):
                    if not in_loop(b):
                        pe.wait_ge(s_exp, j + 1 if is_first(b) else J * (b + 1))
                    source = attn_now[:, j, :] if in_loop(b) else attn[:, b * J + j, :]
                    nc.tensor.transpose(attn_bank(b, j)[0:KEYS, j * P:(j + 1) * P], source,
                                        ident[:]).then_inc(s_eT_ps, 1)

            def weigh_values(b):
                pe.wait_ge(s_v, 1)
                if not is_first(b):
                    pe.wait_ge(s_x2T, b)
                for part in parts(b):
                    pe.wait_ge(s_eT, J * b + part.stop)
                    for j in part:
                        nc.tensor.matmul(value_bank(b, j)[:, j * D:(j + 1) * D], eT[:, j * P:(j + 1) * P], v[:, b, :],
                                         start=True, stop=True).then_inc(s_av, 1)

            def transpose_x2(b):
                pe.wait_ge(s_x2, J * (b + 1))
                for j in range(J):
                    last = nc.tensor.transpose(bank_o[:, j * P:(j + 1) * P], x2[:, j, :], ident[:])
                last.then_inc(s_x2T_ps, 1)

            def transpose_xn(b):
                for part in parts(b):
                    pe.wait_ge(s_xn2, J * b + part.stop)
                    for j in part:
                        nc.tensor.transpose(attn_bank(b, j)[:, j * P:(j + 1) * P], xn2[:, j, :],
                                            ident[:]).then_inc(s_xnT_ps, 1)

            def route(b):
                pe.wait_ge(s_xl, J * (b + 1))
                pe.wait_ge(s_wrlo, 1)
                if not is_first(b):
                    pe.wait_ge(s_combT, b)
                if in_loop(b):
                    pe.wait_ge(s_xr, 2 * (b - 1))
                high, low = (xr[:, 0, :], xr[:, 1, :]) if in_loop(b) else (xh[:, slot(b), :], xl[:, slot(b), :])
                for j in range(J):
                    o = bank_r[:, j * 2 * E:(j + 1) * 2 * E]
                    t = slice(j * P, (j + 1) * P)
                    nc.tensor.matmul(o, high[:, t], wr[:].rearrange("d h e -> d (h e)"), start=True, stop=False)
                    last = nc.tensor.matmul(o[:, 0:E], low[:, t], wr[:, 0, :], start=False, stop=True)
                last.then_inc(s_logit_ps, 1)

            def transpose_comb(b):
                pe.wait_ge(s_comb, b + 1)
                nc.tensor.transpose(bank_r[0:E * J, 0:P], comb[:].rearrange("p e j -> p (e j)"),
                                    ident[:]).then_inc(s_combT_ps, 1)

            def expand(b, s):
                e, h = s // 2, s % 2
                if is_first(b):
                    pe.wait_ge(s_w1lo, e + 1)
                    if s == 1:
                        pe.wait_ge(s_scaled, B - 1)
                if s == 0:
                    pe.wait_ge(s_xl, J * (b + 1))
                for o, at, free, done in ((gate_ps[s % 2], 2 * h, s_silu, s_gate), (up_ps[s % 2], 2 * h + 1, s_y, s_up)):
                    if not is_first(b) or s >= BANKS:
                        pe.wait_ge(free, S * b + s - BANKS + 1)
                    c = slice(at * P, (at + 1) * P)
                    nc.tensor.matmul(o[:], w1_hi[:, e, c], xh[:, slot(b), :], start=True, stop=False)
                    nc.tensor.matmul(o[:], w1_hi[:, e, c], xl[:, slot(b), :], start=False, stop=False)
                    nc.tensor.matmul(o[:], w1_lo[:, e, c], xh[:, slot(b), :], start=False, stop=True).then_inc(done, 1)

            def expand_first():
                gate_at, up_at = slice(0, P), slice(P, 2 * P)
                pe.wait_ge(s_w1lo, 1)
                for part in parts(0):
                    t = slice(part.start * P, part.stop * P)
                    pe.wait_ge(s_xh, part.stop)
                    for o, c in ((gate_ps[0], gate_at), (up_ps[0], up_at)):
                        nc.tensor.matmul(o[:, t], w1_hi[:, 0, c], xh[:, 0, t], start=True, stop=False)
                        nc.tensor.matmul(o[:, t], w1_lo[:, 0, c], xh[:, 0, t], start=False, stop=False)
                    pe.wait_ge(s_xl, part.stop)
                    gate_done = nc.tensor.matmul(gate_ps[0][:, t], w1_hi[:, 0, gate_at], xl[:, 0, t], start=False,
                                                 stop=True)
                    up_done = nc.tensor.matmul(up_ps[0][:, t], w1_hi[:, 0, up_at], xl[:, 0, t], start=False,
                                               stop=True)
                gate_done.then_inc(s_gate, 1)
                up_done.then_inc(s_up, 1)

            def contract(b, s):
                e, h = s // 2, s % 2
                pe.wait_ge(s_yl, S * b + s + 1)
                if is_first(b):
                    pe.wait_ge(s_w2lo, e + 1)
                if s == 0 and not is_first(b):
                    pe.wait_ge(s_final, b)
                c = slice(h * D, (h + 1) * D)
                nc.tensor.matmul(out_ps[:], w2_hi[:, e, c], y_hi[:, s % NS, :], start=s == 0, stop=False)
                nc.tensor.matmul(out_ps[:], w2_hi[:, e, c], y_lo[:, s % NS, :], start=False, stop=False)
                nc.tensor.matmul(out_ps[:], w2_lo[:, e, c], y_hi[:, s % NS, :], start=False,
                                 stop=s == S - 1).then_inc(s_down, 1)

            pe.wait_ge(s_fpack, 16)
            project_keys(0)
            pe.wait_ge(s_wqc, 1)
            fold_query(0)
            score(0)
            pe.wait_ge(s_lpack, 16)
            project_keys(1)
            project_values()
            pe.wait_ge(s_ident, 1)
            transpose_attn(0)
            fold_query(1)
            weigh_values(0)
            score(1)
            pe.wait_ge(s_cbias, 2)
            score(2)
            pe.wait_ge(s_x2, J)
            score(3)
            transpose_x2(0)
            transpose_xn(0)

            def batch(b):
                for s in range(S):
                    if is_first(b) and s == 0:
                        expand_first()
                        route(0)
                    else:
                        expand(b, s)
                    if not is_first(b) or s >= OUT_LAG:
                        contract(*before(b, s, OUT_LAG))
                    if s == (FIRST_COMB_AT if is_first(b) else COMB_AT):
                        transpose_comb(b)
                    if not is_last(b):
                        if s == 1:
                            transpose_attn(b + 1)
                        if s == 3:
                            weigh_values(b + 1)
                        if s == 6:
                            transpose_x2(b + 1)
                        if s == turn_at(b):
                            transpose_xn(b + 1)
                        if s == 11:
                            route(b + 1)

            each_batch(pe, batch)
            for s in range(S - OUT_LAG, S):
                contract(B - 1, s)


def kernel(**inputs):
    import numpy as np
    import concourse.bacc as bacc
    from concourse.bass_utils import run_bass_kernel_spmd

    x = np.asarray(inputs["x"])
    context = np.asarray(inputs["ctx_1024"])
    B, T, D = x.shape
    w1 = np.asarray(inputs["L0_ffn_w1"])
    w2 = np.asarray(inputs["L0_ffn_w2"])
    E = w1.shape[0]
    P = 128
    tokens = x.reshape(B * T, D)
    arrays = {
        "x_rows": tokens.reshape(B * T // P, P, D).transpose(1, 0, 2).reshape(P, -1),
        "x_cols": tokens.T,
        "first_pack": np.concatenate([context[0].T, np.asarray(inputs["L0_xattn_Wk"]).T,
                                      np.asarray(inputs["L0_xattn_bk"])[:, None],
                                      np.asarray(inputs["L0_xattn_bq"])[:, None]], axis=1),
        "wq_rows": np.asarray(inputs["L0_xattn_Wq"]),
        "later_pack": np.concatenate([context[1:].reshape(-1, D).T, np.asarray(inputs["L0_xattn_Wv"]).T,
                                      np.asarray(inputs["L0_ffn_router_w"]).T], axis=1),
        "bv_row": np.asarray(inputs["L0_xattn_bv"])[None, :],
        "w1_cols": w1.reshape(E, 2, 2, P, D).transpose(4, 0, 2, 1, 3).reshape(D, -1),
        "w2_cols": w2.reshape(E, D, 2, P).transpose(3, 0, 2, 1).reshape(P, -1),
    }
    arrays = {name: np.ascontiguousarray(a) for name, a in arrays.items()}

    nc = bacc.Bacc("TRN2", target_bir_lowering=False, num_devices=1)
    args = {name: nc.dram_tensor(name, a.shape, mybir.dt.from_np(a.dtype), kind="ExternalInput").ap()
            for name, a in arrays.items()}
    out = nc.dram_tensor("out", (D, B * T), mybir.dt.float32, kind="ExternalOutput").ap()
    xattn_moe_kernel(nc, out=out, **args)
    r = run_bass_kernel_spmd(nc, [arrays], core_ids=[0])
    return np.ascontiguousarray(r.results[0]["out"].T).reshape(B, T, D)
```
